# Optimizing a Trainium2 kernel written in Bass

```python
import numpy as np
import jax
import jax.numpy as jnp

def _softmax(x, axis=-1):
    return jax.nn.softmax(x, axis=axis)

def _gelu(x):
    return jax.nn.gelu(x, approximate=True)

def _silu(x):
    return jax.nn.silu(x)

def _sigmoid(x):
    return jax.nn.sigmoid(x)

def _layernorm(x, axis=-1, eps=1e-05):
    m = jnp.mean(x, axis=axis, keepdims=True)
    v = jnp.var(x, axis=axis, keepdims=True)
    return (x - m) / jnp.sqrt(v + eps)

def _scatter_add(tgt, idx, src, axis=0):
    return tgt.at[idx].add(src)

def _segment_sum(src, seg, n):
    return jax.ops.segment_sum(src, seg, n)
kernel_name = 'mk_hybrid_d1_jaxref_r8_e87bd2'

def setup_inputs(seed: int=0):
    np.random.seed(seed)
    _w = jnp.asarray

    def _L0_attn_a_setup():
        import jax, jax.numpy as jnp
        import numpy as np
        HIDDEN = 512
        NUM_HEADS = 32
        GROUP_NUM = 8
        HEAD_DIM = HIDDEN // NUM_HEADS
        key = jax.random.key(seed)
        ks = jax.random.split(key, 9)
        s = 0.02
        kv_dim = GROUP_NUM * HEAD_DIM
        return {'hidden_state': jax.random.normal(ks[0], (1, 256, HIDDEN), dtype=jnp.float32), 'wq': jax.random.normal(ks[1], (HIDDEN, HIDDEN), dtype=jnp.float32) * s, 'bq': jnp.zeros((HIDDEN,), dtype=jnp.float32), 'wk': jax.random.normal(ks[2], (HIDDEN, kv_dim), dtype=jnp.float32) * s, 'bk': jnp.zeros((kv_dim,), dtype=jnp.float32), 'wv': jax.random.normal(ks[3], (HIDDEN, kv_dim), dtype=jnp.float32) * s, 'bv': jnp.zeros((kv_dim,), dtype=jnp.float32), 'wo': jax.random.normal(ks[4], (HIDDEN, HIDDEN), dtype=jnp.float32) * s, 'bo': jnp.zeros((HIDDEN,), dtype=jnp.float32)}
    _L0_attn_a_in = _L0_attn_a_setup()

    def _L0_attn_b_setup():
        import jax, jax.numpy as jnp
        import numpy as np
        import math
        B, S, H = (1, 256, 512)
        NH, NKV, HD = (32, 8, 128)
        GS = 128
        WBITS = 4
        ZERO = float(2 ** (WBITS - 1))
        THETA = 10000.0

        def _dequant_matmul(x, qw, scales):
            w = (qw.astype(jnp.float32) - ZERO) * jnp.repeat(scales, GS, axis=0)
            return x @ w

        def _rope_tables(seq_len, dtype):
            inv_freq = 1.0 / THETA ** (jnp.arange(0, HD, 2, dtype=jnp.float32) / HD)
            freqs = jnp.arange(seq_len, dtype=jnp.float32)[:, None] * inv_freq
            emb = jnp.concatenate([freqs, freqs], axis=-1)
            return (jnp.cos(emb).astype(dtype), jnp.sin(emb).astype(dtype))

        def _rotate_half(x):
            x1, x2 = jnp.split(x, 2, axis=-1)
            return jnp.concatenate([-x2, x1], axis=-1)

        def _apply_rope(x, cos, sin):
            return x * cos[None, None] + _rotate_half(x) * sin[None, None]
        key = jax.random.key(seed)
        ks = jax.random.split(key, 9)
        small = lambda k, shp: jax.random.uniform(k, shp, jnp.float32) * 0.01 + 0.001
        return {'hidden_states': jax.random.normal(ks[0], (B, S, H), jnp.float32), 'scales_q': small(ks[1], (H // GS, NH * HD)), 'scales_k': small(ks[2], (H // GS, NKV * HD)), 'scales_v': small(ks[3], (H // GS, NKV * HD)), 'scales_o': small(ks[4], (NH * HD // GS, H)), 'qw_q': jax.random.randint(ks[5], (H, NH * HD), 0, 2 ** WBITS, jnp.int32), 'qw_k': jax.random.randint(ks[6], (H, NKV * HD), 0, 2 ** WBITS, jnp.int32), 'qw_v': jax.random.randint(ks[7], (H, NKV * HD), 0, 2 ** WBITS, jnp.int32), 'qw_o': jax.random.randint(ks[8], (NH * HD, H), 0, 2 ** WBITS, jnp.int32)}
    _L0_attn_b_in = _L0_attn_b_setup()

    def _L0_ffn_setup():
        import jax, jax.numpy as jnp
        import numpy as np
        NUM_EXPERTS = 8
        TOP_K = 2
        RANK = 16
        LORA_ALPHA = 32
        SCALING = LORA_ALPHA / RANK
        key = jax.random.key(seed)
        ks = jax.random.split(key, 6)
        B, S, D_IN, D_OUT = (4, 256, 512, 512)
        x = jax.random.normal(ks[0], (B, S, D_IN), dtype=jnp.float32)
        W_base = jax.random.normal(ks[1], (D_OUT, D_IN), dtype=jnp.float32) * 0.02
        b_base = jax.random.normal(ks[2], (D_OUT,), dtype=jnp.float32) * 0.02
        W_router = jax.random.normal(ks[3], (NUM_EXPERTS, D_IN), dtype=jnp.float32) * 0.02
        A = jax.random.normal(ks[4], (NUM_EXPERTS, RANK, D_IN), dtype=jnp.float32) * 0.02
        Bm = jax.random.normal(ks[5], (D_OUT, RANK), dtype=jnp.float32) * 0.02
        Bm = jnp.broadcast_to(Bm, (NUM_EXPERTS, D_OUT, RANK)) * jnp.arange(1, NUM_EXPERTS + 1, dtype=jnp.float32)[:, None, None] * 0.2
        return {'x': x, 'W_base': W_base, 'b_base': b_base, 'W_router': W_router, 'A': A, 'B': Bm}
    _L0_ffn_in = _L0_ffn_setup()
    _d = {'L0_attn_a_hidden_state': _L0_attn_a_in['hidden_state'], 'L0_attn_a_wq': _L0_attn_a_in['wq'], 'L0_attn_a_bq': _L0_attn_a_in['bq'], 'L0_attn_a_wk': _L0_attn_a_in['wk'], 'L0_attn_a_bk': _L0_attn_a_in['bk'], 'L0_attn_a_wv': _L0_attn_a_in['wv'], 'L0_attn_a_bv': _L0_attn_a_in['bv'], 'L0_attn_a_wo': _L0_attn_a_in['wo'], 'L0_attn_a_bo': _L0_attn_a_in['bo'], 'L0_attn_b_scales_q': _L0_attn_b_in['scales_q'], 'L0_attn_b_scales_k': _L0_attn_b_in['scales_k'], 'L0_attn_b_scales_v': _L0_attn_b_in['scales_v'], 'L0_attn_b_scales_o': _L0_attn_b_in['scales_o'], 'L0_attn_b_qw_q': _L0_attn_b_in['qw_q'], 'L0_attn_b_qw_k': _L0_attn_b_in['qw_k'], 'L0_attn_b_qw_v': _L0_attn_b_in['qw_v'], 'L0_attn_b_qw_o': _L0_attn_b_in['qw_o'], 'L0_ffn_W_base': _L0_ffn_in['W_base'], 'L0_ffn_b_base': _L0_ffn_in['b_base'], 'L0_ffn_W_router': _L0_ffn_in['W_router'], 'L0_ffn_A': _L0_ffn_in['A'], 'L0_ffn_B': _L0_ffn_in['B']}
    _x0 = _d['L0_attn_a_hidden_state']
    _d['L0_attn_a_hidden_state'] = jax.random.normal(jax.random.fold_in(jax.random.key(seed), 1), (1, 1024, 512), dtype=_x0.dtype)
    del _x0
    return _d

def reference(L0_attn_a_hidden_state, L0_attn_a_wq, L0_attn_a_bq, L0_attn_a_wk, L0_attn_a_bk, L0_attn_a_wv, L0_attn_a_bv, L0_attn_a_wo, L0_attn_a_bo, L0_attn_b_scales_q, L0_attn_b_scales_k, L0_attn_b_scales_v, L0_attn_b_scales_o, L0_attn_b_qw_q, L0_attn_b_qw_k, L0_attn_b_qw_v, L0_attn_b_qw_o, L0_ffn_W_base, L0_ffn_b_base, L0_ffn_W_router, L0_ffn_A, L0_ffn_B):

    def _L0_attn_a_ref(hidden_state, wq, bq, wk, bk, wv, bv, wo, bo):
        import jax, jax.numpy as jnp
        import numpy as np
        HIDDEN = 512
        NUM_HEADS = 32
        GROUP_NUM = 8
        HEAD_DIM = HIDDEN // NUM_HEADS
        B, S, _ = hidden_state.shape
        q = hidden_state @ wq + bq
        k = hidden_state @ wk + bk
        v = hidden_state @ wv + bv
        q = q.reshape(B, S, NUM_HEADS, HEAD_DIM).transpose(0, 2, 1, 3)
        k = k.reshape(B, S, GROUP_NUM, HEAD_DIM).transpose(0, 2, 1, 3)
        v = v.reshape(B, S, GROUP_NUM, HEAD_DIM).transpose(0, 2, 1, 3)
        rep = NUM_HEADS // GROUP_NUM
        k = jnp.repeat(k, rep, axis=1)
        v = jnp.repeat(v, rep, axis=1)
        scale = 1.0 / jnp.sqrt(jnp.float32(HEAD_DIM))
        scores = jnp.einsum('bhqd,bhkd->bhqk', q, k) * scale
        probs = jax.nn.softmax(scores, axis=-1)
        out = jnp.einsum('bhqk,bhkd->bhqd', probs, v)
        out = jnp.swapaxes(out, -1, -2).reshape(B, -1, HEAD_DIM * NUM_HEADS)
        return out @ wo + bo

    def _L0_attn_b_ref(hidden_states, scales_q, scales_k, scales_v, scales_o, qw_q, qw_k, qw_v, qw_o):
        import jax, jax.numpy as jnp
        import numpy as np
        import math
        B, S, H = (1, 256, 512)
        NH, NKV, HD = (32, 8, 128)
        GS = 128
        WBITS = 4
        ZERO = float(2 ** (WBITS - 1))
        THETA = 10000.0

        def _dequant_matmul(x, qw, scales):
            w = (qw.astype(jnp.float32) - ZERO) * jnp.repeat(scales, GS, axis=0)
            return x @ w

        def _rope_tables(seq_len, dtype):
            inv_freq = 1.0 / THETA ** (jnp.arange(0, HD, 2, dtype=jnp.float32) / HD)
            freqs = jnp.arange(seq_len, dtype=jnp.float32)[:, None] * inv_freq
            emb = jnp.concatenate([freqs, freqs], axis=-1)
            return (jnp.cos(emb).astype(dtype), jnp.sin(emb).astype(dtype))

        def _rotate_half(x):
            x1, x2 = jnp.split(x, 2, axis=-1)
            return jnp.concatenate([-x2, x1], axis=-1)

        def _apply_rope(x, cos, sin):
            return x * cos[None, None] + _rotate_half(x) * sin[None, None]
        b, s, _ = hidden_states.shape
        q = _dequant_matmul(hidden_states, qw_q, scales_q).reshape(b, s, NH, HD).transpose(0, 2, 1, 3)
        k = _dequant_matmul(hidden_states, qw_k, scales_k).reshape(b, s, NKV, HD).transpose(0, 2, 1, 3)
        v = _dequant_matmul(hidden_states, qw_v, scales_v).reshape(b, s, NKV, HD).transpose(0, 2, 1, 3)
        cos, sin = _rope_tables(s, hidden_states.dtype)
        q = _apply_rope(q, cos, sin)
        k = _apply_rope(k, cos, sin)
        rep = NH // NKV
        k = jnp.repeat(k, rep, axis=1)
        v = jnp.repeat(v, rep, axis=1)
        scores = jnp.einsum('bhqd,bhkd->bhqk', q, k) / math.sqrt(HD)
        causal = jnp.tril(jnp.ones((s, s), dtype=bool))
        scores = jnp.where(causal[None, None], scores, jnp.finfo(scores.dtype).min)
        attn = jax.nn.softmax(scores.astype(jnp.float32), axis=-1).astype(q.dtype)
        ctx = jnp.einsum('bhqk,bhkd->bhqd', attn, v)
        ctx = ctx.transpose(0, 2, 1, 3).reshape(b, s, NH * HD)
        return _dequant_matmul(ctx, qw_o, scales_o)

    def _L0_ffn_ref(x, W_base, b_base, W_router, A, B):
        import jax, jax.numpy as jnp
        import numpy as np
        NUM_EXPERTS = 8
        TOP_K = 2
        RANK = 16
        LORA_ALPHA = 32
        SCALING = LORA_ALPHA / RANK
        bs, seq, d_in = x.shape
        T = bs * seq
        xf = x.reshape(T, d_in)
        base = xf @ W_base.T + b_base
        logits = xf @ W_router.T
        rw, sel = jax.lax.top_k(logits, TOP_K)
        rw = jax.nn.softmax(rw, axis=-1)
        onehot = jax.nn.one_hot(sel, NUM_EXPERTS, dtype=rw.dtype)
        w = jnp.einsum('tk,tke->te', rw, onehot)
        h = jnp.einsum('td,erd->ter', xf, A)
        lora = jnp.einsum('ter,te,eor->to', h, w, B) * SCALING
        return (base + lora).reshape(bs, seq, -1)
    x = L0_attn_a_hidden_state
    x = x + _L0_attn_a_ref(_layernorm(x, axis=-1), L0_attn_a_wq, L0_attn_a_bq, L0_attn_a_wk, L0_attn_a_bk, L0_attn_a_wv, L0_attn_a_bv, L0_attn_a_wo, L0_attn_a_bo)
    x = x + _L0_ffn_ref(_layernorm(x, axis=-1), L0_ffn_W_base, L0_ffn_b_base, L0_ffn_W_router, L0_ffn_A, L0_ffn_B)
    x = x + _L0_attn_b_ref(_layernorm(x, axis=-1), L0_attn_b_scales_q, L0_attn_b_scales_k, L0_attn_b_scales_v, L0_attn_b_scales_o, L0_attn_b_qw_q, L0_attn_b_qw_k, L0_attn_b_qw_v, L0_attn_b_qw_o)
    x = x + _L0_ffn_ref(_layernorm(x, axis=-1), L0_ffn_W_base, L0_ffn_b_base, L0_ffn_W_router, L0_ffn_A, L0_ffn_B)
    return x

_drawn_inputs = setup_inputs


def setup_inputs(seed=0):
    import zlib

    import numpy as np

    out = dict(_drawn_inputs(seed))
    spreads = {'L0_attn_a_bq': (0.0, 0.8),
     'L0_attn_a_bk': (0.0, 0.8),
     'L0_attn_a_bv': (0.0, 0.1),
     'L0_attn_a_bo': (0.0, 0.1)}
    factors = {'L0_attn_a_wq': 8.0,
     'L0_attn_a_wk': 8.0,
     'L0_attn_a_wv': 7.899,
     'L0_attn_b_scales_q': 3.014,
     'L0_attn_b_scales_k': 2.937}
    for name, (base, spread) in spreads.items():
        noise = np.random.default_rng([zlib.crc32(name.encode()), seed]).standard_normal(out[name].shape)
        drawn = base * np.exp(spread * noise) if base else spread * noise
        out[name] = jnp.asarray(drawn.astype(out[name].dtype))
    for name, factor in factors.items():
        out[name] = (out[name] * factor).astype(out[name].dtype)
    return out
```

```python
from contextlib import ExitStack

import numpy as np

import concourse.bass as bass
from concourse import mybir

P = 128
S = 1024
D = 512
T = S // P
KC = D // P
HALF = S // 2

NH = 32
G = 8
R = NH // G
HD = D // NH
K_PART = (0, 0, 1, 0, 1, 2)
Q_PART = (0, 1, 0, 2, 1, 0)
STACK = HD * len(K_PART)
NEG = 3
KT = S // P
MM = R * (HALF // P) * 2
VW = 32

BW = R * P + 2 * P
BH = R + 1
SC_B = float(P) ** -0.5
ZERO = 8.0

NE = 8
RANK = 16
ER = NE * RANK
SCALING = 2.0
EPS = 1e-5

F32 = mybir.dt.float32
BF16 = mybir.dt.bfloat16
I32 = mybir.dt.int32
U32 = mybir.dt.uint32
ALU = mybir.AluOpType
ACT = mybir.ActivationFunctionType
AX = mybir.AxisListType
ds = bass.ds


def build(nc, x_d, wq_d, bq_d, wk_d, bk_d, wv_d, bv_d, wo_d, bo_d,
          sq_d, sk_d, sv_d, so_d, qq_d, qk_d, qv_d, qo_d,
          wb_d, bb_d, wr_d, a_d, b_d, ident_d, cos_d, sin_d, mask_d, out_d, stop=9):
    x_nat = x_d.rearrange("o (t p) d -> (o t) p d", p=P)
    x_il = x_d.rearrange("o (b p f) d -> p (o b) f d", p=P, f=2)
    out_il = out_d.rearrange("o (b p f) d -> p (o b) f d", p=P, f=2)
    out_nat = out_d.rearrange("o (t p) d -> (o t) p d", p=P)

    with ExitStack() as ctx:
        def sb(name, shape, dt=F32):
            return ctx.enter_context(nc.sbuf_tensor(name, shape, dt))

        def sem(name):
            return ctx.enter_context(nc.semaphore(name))

        x = sb("x", [P, T, D])
        xnat = sb("xnat", [P, T, D])
        xT = sb("xT", [P, KC, S])
        ident = sb("ident", [P, P])
        identb = sb("identb", [P, P], BF16)
        wbT = sb("wbT", [P, KC, D])
        wrT = sb("wrT", [P, KC, NE])
        aT = sb("aT", [P, KC, ER])
        bT = sb("bT", [P, D])
        bb = sb("bb", [P, D])
        xh = sb("xh", [P, 2, D])
        stats = sb("stats", [P, T, 6])
        mv = sb("mv", [P, T, 2])
        nrm = sb("nrm", [P, 6, T])
        hid = sb("hid", [P, 2, ER])
        hidT = sb("hidT", [P, 2, P])
        iota8 = sb("iota8", [P, NE])
        iota8i = sb("iota8i", [P, NE], I32)
        rt8 = sb("rt8", [P, 2, 2, NE])
        rti = sb("rti", [P, 2, NE], U32)
        rts = sb("rts", [P, 2, 8])

        ARENA = 33280
        arena = sb("arena", [P, ARENA])
        top = [0]

        def carve(words, dt=F32):
            a = arena[:, top[0]:top[0] + words]
            top[0] += words
            assert top[0] <= ARENA, top[0]
            return a.bitcast(dt) if dt != F32 else a

        wq = carve(KC * D).rearrange("p (k n) -> p k n", k=KC)
        wkv = carve(KC * 2 * P).rearrange("p (k n) -> p k n", k=KC)
        q32 = carve(S)
        pbuf = arena[:, 0:4 * S].rearrange("p (b n) -> p b n", b=4)
        at_parts = top[0]
        r32 = carve(S)
        parts = carve(2 * 3 * S // 2, BF16).rearrange("p (b c n) -> p b c n", b=2, c=3)
        oall = arena[:, at_parts:at_parts + T * D].rearrange("p (t n) -> p t n", t=T)
        qs = carve(NH * S // 2, BF16).rearrange("p (h n) -> p h n", h=NH)
        ks = carve(G * S // 2, BF16).rearrange("p (g n) -> p g n", g=G)
        vx = carve(KT * G * VW).rearrange("p (t g w) -> p t g w", t=KT, g=G)
        vcur = carve(KT * VW).rearrange("p (t w) -> p t w", t=KT)
        osb = carve(HALF)
        mx = carve(2 * MM).rearrange("p (f i h) -> p f i h", f=2, h=2)
        nm = carve(MM).rearrange("p (c i) -> p c i", c=2)
        mparts = carve(MM, BF16).rearrange("p (i c) -> p i c", c=4)
        rc = carve(16).rearrange("p (t j) -> p t j", t=4)
        bqk = carve(8)
        bv = carve(P)
        bo = carve(D)
        wo = xT[:, 0:2, :].rearrange("p a (b n) -> p (a b) n", b=2)
        raw = x[:, 0:KC, :]

        top[0] = 0
        wg = [carve(KC * BW).rearrange("p (k n) -> p k n", k=KC) for _ in range(2)]
        wog = [carve(R * D).rearrange("p (h n) -> p h n", h=R) for _ in range(2)]
        stq = carve(KC * BW).rearrange("p (k n) -> p k n", k=KC)
        scq = carve(KC * BW).rearrange("p (k n) -> p k n", k=KC)
        sto = carve(R * D).rearrange("p (h n) -> p h n", h=R)
        sco = carve(R * D).rearrange("p (h n) -> p h n", h=R)
        qT = carve(R * P).rearrange("p (h n) -> p h n", h=R)
        kT = carve(S)
        vB = [carve(S).rearrange("p (t d) -> p t d", t=T) for _ in range(2)]
        pr = carve(R * S).rearrange("p (h n) -> p h n", h=R)
        pT = x
        cT = carve(R * P).rearrange("p (h n) -> p h n", h=R)
        rc1 = carve(BH * P)
        rc2 = carve(BH * P)
        cos = carve(T * P).rearrange("p (t d) -> p t d", t=T)
        sin = carve(T * P).rearrange("p (t d) -> p t d", t=T)
        mask = carve(P // 2, BF16)
        mxb = carve(R)
        nmb = carve(R)
        den = carve(R)
        rden = carve(R)

        ps = ctx.enter_context(nc.psum_tensor("ps", [P, 8, 512], F32))
        scratch = nc.dram_tensor("scratch", (5, 3, P, S), BF16, kind="Internal").ap()

        s_x = [sem(f"s_x{t}") for t in range(T)]
        s_wqkv = sem("s_wqkv")
        s_xr = sem("s_xr")
        s_wo = sem("s_wo")
        s_cst = sem("s_cst")
        s_raw = sem("s_raw")
        s_rawa = sem("s_rawa")
        s_idb = sem("s_idb")
        s_set = sem("s_set")
        s_st = sem("s_stats")
        s_sq = sem("s_sqrt")
        s_xh = sem("s_xh")
        s_lntr = sem("s_lntr")
        s_xt = sem("s_xt")
        s_qk = sem("s_qk")
        s_q32 = sem("s_q32")
        s_r1 = sem("s_r1")
        s_p2 = sem("s_p2")
        s_p3 = sem("s_p3")
        s_stk = [sem(f"s_stk{j}") for j in range(5)]
        s_scr = [sem(f"s_scr{n}") for n in range(5)]
        s_v = sem("s_v")
        s_vx = sem("s_vx")
        s_wt = sem("s_wt")
        s_we = sem("s_we")
        s_mm = sem("s_mm")
        s_mx = sem("s_mx")
        s_ch = sem("s_ch")
        s_rt = sem("s_rt")
        s_rw = sem("s_rw")
        s_sT = sem("s_sT")
        s_ex = sem("s_ex")
        s_vc = sem("s_vc")
        s_pv = sem("s_pv")
        s_ob = sem("s_ob")
        s_ot = sem("s_ot")
        s_on = sem("s_on")
        s_rec = sem("s_rec")
        s_wom = sem("s_wom")
        s_xa = sem("s_xa")
        s_xb = sem("s_xb")
        s_fh = sem("s_fh")
        s_fd = sem("s_fd")
        s_fe = sem("s_fe")
        s_hw = sem("s_hw")
        s_ft = sem("s_ft")
        s_fc = sem("s_fc")
        s_fy = sem("s_fy")
        s_fx = sem("s_fx")
        s_dve = sem("s_dve")
        s_nat = sem("s_nat")
        s_out = sem("s_out")
        s_tab = sem("s_tab")
        s_wl = [sem("s_wl0"), sem("s_wl1")]
        s_dq = sem("s_dq")
        s_pj = sem("s_pj")
        s_rope = sem("s_rope")
        s_rpa = sem("s_rpa")
        s_vb = sem("s_vb")
        s_qkT = sem("s_qkT")
        s_qke = sem("s_qke")
        s_sc = sem("s_sc")
        s_mb = sem("s_mb")
        s_nb = sem("s_nb")
        s_eb = sem("s_eb")
        s_rd = sem("s_rd")
        s_pn = sem("s_pn")
        s_pt = sem("s_pt")
        s_pta = sem("s_pta")
        s_ptd = sem("s_ptd")
        s_pvb = sem("s_pvb")
        s_cx = sem("s_cx")
        s_op = sem("s_op")
        s_xo = sem("s_xo")

        def flat(bank, n):
            return ps[:, bank:bank + 2, :].rearrange("p b n -> p (b n)")[:, 0:n]

        CHUNKS = {0: (), 1: (), 2: (), 3: (0,), 4: (1, 2), 5: (3, 4), 6: (5, 6), 7: (7,)}

        def act_moves(t):
            return (t + 2) // 2

        def dve_moves(t):
            return (t + 1) // 2

        ACT_PER_G = sum(act_moves(t) for t in range(T))
        DVE_PER_G = sum(dve_moves(t) for t in range(T))
        PT_PER_G = sum(t + 1 for t in range(T))

        def before(moves, t):
            return sum(moves(i) for i in range(t))

        block = ctx.enter_context(nc.Block())


        @block.sync
        def _(sp):
            for t in range(T):
                sp.dma_start(xnat[:, t, :], x_nat[t]).then_inc(s_x[t], 16)
                if t == 0:
                    sp.dma_start(ident[:], ident_d).then_inc(s_cst, 16)
            sp.dma_start(wkv[:, :, 0:P], wk_d.rearrange("(k p) n -> p k n", p=P)).then_inc(s_wqkv, 16)
            sp.dma_start(bqk[:, 0:4], bq_d.rearrange("(j p) -> p j", p=P), allow_slow_non_contiguous=True).then_inc(s_wqkv, 16)
            sp.dma_start(bqk[:, 4:5], bk_d.rearrange("(j p) -> p j", p=P), allow_slow_non_contiguous=True).then_inc(s_wqkv, 16)
            sp.dma_start(wq, wq_d.rearrange("(k p) n -> p k n", p=P)).then_inc(s_wqkv, 16)
            sp.dma_start(wkv[:, :, P:], wv_d.rearrange("(k p) n -> p k n", p=P)).then_inc(s_wqkv, 16)
            sp.dma_start(bv, bv_d.partition_broadcast(P)).then_inc(s_wqkv, 16)
            sp.dma_start(raw, wb_d.rearrange("(t p) d -> p t d", p=P)).then_inc(s_raw, 16)
            for n, j in enumerate((4, 0, 1, 2, 3)):
                sp.wait_ge(s_p2, n + 1)
                sp.wait_ge(s_p3, n + 1)
                sp.dma_start(scratch[n].rearrange("c p n -> p c n"), parts[:, n % 2]).then_inc(s_scr[n], 16)
                sp.wait_ge(s_scr[n], 16)
                for b in range(len(K_PART)):
                    rows = slice(HD * b, HD * b + HD)
                    dst, part = (ks[rows], K_PART[b]) if j == 4 else (qs[rows, 8 * j:8 * j + 8, :], Q_PART[b])
                    sp.dma_start(dst, scratch[n, part].rearrange("(h d) n -> d h n", d=HD)).then_inc(s_stk[j], 16)
            sp.wait_ge(s_wt, KC)
            sp.dma_start(raw[:, 0, :], a_d.rearrange("e r d -> (e r) d")).then_inc(s_rawa, 16)
            sp.dma_start(raw[0:NE, 1, :], wr_d).then_inc(s_rawa, 16)
            for t in range(KC):
                sp.dma_start(raw[:, 2, t * ER:(t + 1) * ER].rearrange("p (e r) -> p e r", r=RANK),
                             b_d[:, t * P:(t + 1) * P, :].rearrange("e o r -> o e r")).then_inc(s_rawa, 16)
            sp.wait_ge(s_qk, 5)
            sp.wait_ge(s_v, 2)
            sp.dma_start(wo, wo_d.rearrange("(k p) n -> p k n", p=P)).then_inc(s_wo, 16)
            sp.wait_ge(s_wt, KC + 3)
            for b in range(T // 2):
                sp.dma_start(x[:, 2 * b:2 * b + 2, :], x_il[:, b]).then_inc(s_xr, 16)
            sp.dma_start(bo, bo_d.partition_broadcast(P)).then_inc(s_xr, 16)
            sp.dma_start(bb[:], bb_d.partition_broadcast(P)).then_inc(s_xr, 16)

            if stop == 1:
                sp.wait_ge(s_xa, T)
                for b in range(T // 2):
                    sp.dma_start(out_il[:, b], x[:, 2 * b:2 * b + 2, :]).then_inc(s_out, 32)
                sp.wait_ge(s_out, 16 * T)
                return

            sp.wait_ge(s_xa, T)
            sp.dma_start(cos, cos_d.rearrange("(t p) d -> p t d", p=P)).then_inc(s_tab, 16)
            sp.dma_start(sin, sin_d.rearrange("(t p) d -> p t d", p=P)).then_inc(s_tab, 16)
            sp.dma_start(rc2[:, 0:P], mask_d).then_inc(s_tab, 16)

            def load_group(g):
                sp.dma_start(stq[:, :, 0:R * P].bitcast(I32),
                             qq_d[:, ds(g * (R * P), R * P)].rearrange("(k p) n -> p k n", p=P)).then_inc(s_wl[0], 16)
                sp.dma_start(scq[:, :, 0:R * P],
                             sq_d[:, ds(g * (R * P), R * P)].partition_broadcast(P)).then_inc(s_wl[0], 16)
                for c, w_d, s_d in ((R * P, qk_d, sk_d), (R * P + P, qv_d, sv_d)):
                    sp.dma_start(stq[:, :, c:c + P].bitcast(I32),
                                 w_d[:, ds(g * P, P)].rearrange("(k p) n -> p k n", p=P)).then_inc(s_wl[0], 16)
                    sp.dma_start(scq[:, :, c:c + P], s_d[:, ds(g * P, P)].partition_broadcast(P)).then_inc(s_wl[0], 16)
                sp.dma_start(sto.bitcast(I32),
                             qo_d[ds(g * (R * P), R * P), :].rearrange("(h p) n -> p h n", p=P)).then_inc(s_wl[1], 16)
                sp.dma_start(sco, so_d[ds(g * R, R), :].partition_broadcast(P)).then_inc(s_wl[1], 16)

            load_group(0)
            sp.wait_ge(s_fx, T)
            for t in range(T):
                for f in range(2):
                    sp.dma_start(xnat[f:P:2, t, :],
                                 x[HALF // 8 * (t % 2):HALF // 8 * (t % 2) + HALF // 8, 2 * (t // 2) + f, :]).then_inc(s_nat, 16)
            if stop == 2:
                sp.wait_ge(s_nat, 32 * T)
                for t in range(T):
                    sp.dma_start(out_nat[t], xnat[:, t, :]).then_inc(s_out, 16)
                sp.wait_ge(s_out, 16 * T)
                return
            with sp.Fori(0, G - 1) as g:
                sp.wait_ge(s_dq, g * 8 + 8)
                load_group(g + 1)
            for t in range(T):
                sp.wait_ge(s_fx, T + t + 1)
                sp.dma_start(out_nat[t], xnat[:, t, :]).then_inc(s_out, 16)
            sp.wait_ge(s_out, 16 * T)

        @block.gpsimd
        def _(pool):
            pool.iota(iota8i[:], pattern=[[1, NE]], base=0, channel_multiplier=0).then_inc(s_set, 1)
            pool.memset(vx, 0.0).then_inc(s_set, 1)
            pool.wait_ge(s_set, 2)
            pool.memset(ks[STACK:STACK + NEG], 1.0).then_inc(s_set, 1)
            pool.wait_ge(s_set, 3)
            pool.memset(vx[:, :, :, HD:HD + 1], 1.0).then_inc(s_set, 1)
            pool.tensor_copy(iota8[:], iota8i[:]).then_inc(s_set, 1)
            for n in range(5):
                pool.wait_ge(s_r1, n + 1)
                pool.tensor_copy(parts[:, n % 2, 1, :], r32).then_inc(s_p2, 1)
            pool.wait_ge(s_xr, 16 * 6)
            for t in range(T):
                pool.tensor_tensor(x[:, t, :], x[:, t, :], bo, ALU.add).then_inc(s_xb, 1)
            pool.wait_ge(s_vx, 2)
            pool.tensor_copy(vcur, vx[:, :, 0, :]).then_inc(s_vc, 1)
            with pool.Fori(1, G) as g:
                pool.wait_ge(s_pv, g * (2 * KT))
                pool.tensor_copy(vcur, vx[:, :, ds(g, 1), :].rearrange("p t g w -> p t (g w)")).then_inc(s_vc, 1)
            if stop == 1:
                return

            def add_base_bias(buf, phase):
                for t in range(T):
                    pool.wait_ge(s_xh, T * phase + t + 1)
                    pool.tensor_tensor(buf[:, t, :], buf[:, t, :], bb[:], ALU.add).then_inc(s_xb, 1)

            add_base_bias(x, 1)
            if stop == 2:
                return

            def rope_add(v):
                pool.wait_ge(s_rope, v * 3 + 3)
                pool.tensor_tensor(rc1, rc1, rc2, ALU.add).then_inc(s_rpa, 1)

            def group(g, last):
                for t in range(T - 1 if last else T):
                    rope_add(g * T + t + 1)

            rope_add(0)
            with pool.Fori(0, G - 1) as g:
                group(g, False)
            group(G - 1, True)
            add_base_bias(xnat, 3)

        @block.scalar
        def _(act):
            def norm(phase):
                act.wait_ge(s_st, phase + 1)
                nc.scalar.activation(nrm[:, 1, :], nrm[:, 0, :], ACT.Sqrt).then_inc(s_sq, 1)
                for t in range(T):
                    i = T * phase + t
                    act.wait_ge(s_lntr, i + 1)
                    nc.scalar.activation(xT[:, :, t * P:(t + 1) * P],
                                         ps[:, i % 2, :].rearrange("p (k n) -> p k n", k=KC), ACT.Copy).then_inc(s_xt, 1)

            norm(0)
            act.wait_ge(s_wqkv, 16 * 6)
            for n, j in enumerate((4, 0, 1, 2, 3)):
                b = 2 + 2 * (n % 2)
                act.wait_ge(s_qk, n + 1)
                if n >= 1:
                    act.wait_ge(s_r1, n)
                nc.scalar.activation(q32.rearrange("p (b n) -> p b n", b=2), ps[:, b:b + 2, :], ACT.Identity,
                                     bias=bqk[:, j:j + 1]).then_inc(s_q32, 1)
                if n >= 2:
                    act.wait_ge(s_scr[n - 2], 16)
                nc.scalar.activation(parts[:, n % 2, 0, :].rearrange("p (b n) -> p b n", b=2), ps[:, b:b + 2, :],
                                     ACT.Identity, bias=bqk[:, j:j + 1]).then_inc(s_q32, 1)

            def row_copy(v, r):
                g, f = v
                n = (g * 2 + f) * 2 + r
                act.wait_ge(s_rt, n + 1)
                nc.scalar.activation(
                    qs[STACK:STACK + NEG, ds(g * R + 2 * r, 2), f * HALF:(f + 1) * HALF],
                    ps[STACK:STACK + NEG, 2, :].bitcast(BF16).rearrange("p (h n) -> p h n", h=2),
                    ACT.Copy).then_inc(s_rw, 1)

            def o_copy(u):
                act.wait_ge(s_pv, u * KT + KT)
                nc.scalar.activation(osb, ps[:, 3, :], ACT.Copy).then_inc(s_ob, 1)

            def exps(g, last):
                for f in range(2):
                    u = g * 2 + f
                    for e in range(2 * KT):
                        act.wait_ge(s_sT, u * (2 * KT) + e + 1)
                        if f == 1 or e >= 4:
                            act.wait_ge(s_pv, u * KT + e // 2 - 1)
                        b = 4 + 2 * (e % 2)
                        nc.scalar.activation(pbuf[:, e % 4, :].rearrange("p (b n) -> p b n", b=2), ps[:, b:b + 2, :],
                                             ACT.Exp, scale=float(HD) ** -0.5).then_inc(s_ex, 1)
                        if f == 1 and e == 1:
                            o_copy(g * 2)
                        if e in (8, 10) and not (last and f == 1):
                            row_copy((g + f, 1 - f), (e - 8) // 2)
                o_copy(g * 2 + 1)

            for r in range(2):
                row_copy((0, 0), r)
            with act.Fori(0, G - 1) as g:
                exps(g, False)
            exps(G - 1, True)
            if stop == 1:
                return
            norm(1)

            def mixture(q):
                for t in range(T):
                    i = T * q + t
                    act.wait_ge(s_fd, i + 1)
                    nc.scalar.activation(rts[:, t % 2, 1:2], rts[:, t % 2, 0:1], ACT.Exp).then_inc(s_fe, 1)
                    act.wait_ge(s_ft, i + 1)
                    nc.scalar.activation(hidT[:, t % 2, :], ps[:, 6, 0:P], ACT.Copy).then_inc(s_fc, 1)

            mixture(0)
            if stop == 2:
                return
            norm(2)

            def values(v, par, t):
                act.wait_ge(s_pj, v + 1)
                nc.scalar.activation(vB[par][:, t, :], ps[:, 7, P:2 * P], ACT.Copy).then_inc(s_vb, 1)

            def turned(v, t):
                act.wait_ge(s_qkT, v + 1)
                nc.scalar.activation(qT.rearrange("p h n -> p (h n)"), ps[:, 1, :], ACT.Copy).then_inc(s_qke, 1)
                nc.scalar.activation(kT[:, t * P:(t + 1) * P], ps[:, 3, 0:P], ACT.Copy).then_inc(s_qke, 1)

            def group_b(g, par, last):
                for t in range(T):
                    u = g * T + t
                    n = (t + 1) * P
                    for h in range(R):
                        act.wait_ge(s_nb, u * R + h + 1)
                        nc.scalar.activation(pr[:, h, 0:n], flat(2 * (h % 2), n), ACT.Exp, bias=nmb[:, h:h + 1],
                                             scale=SC_B, accum_out=den[:, h:h + 1]).then_inc(s_eb, 1)
                    end = last and t == T - 1
                    if not end:
                        values(u + 1, par if t < T - 1 else 1 - par, (t + 1) % T)
                    for kt in range(0, t + 1, 2):
                        act.wait_ge(s_pt, g * PT_PER_G + before(lambda i: i + 1, t) + kt + 1)
                        nc.scalar.activation(pT[:, kt, :], ps[:, 4, :], ACT.Copy).then_inc(s_pta, 1)
                    act.wait_ge(s_pvb, u + 1)
                    nc.scalar.activation(cT.rearrange("p h n -> p (h n)"), ps[:, 0, :], ACT.Copy).then_inc(s_cx, 1)
                    if not end:
                        turned(u + 1, (t + 1) % T)

            values(0, 0, 0)
            turned(0, 0)
            with act.Fori(0, G // 2 - 1) as gg:
                group_b(gg * 2, 0, False)
                group_b(gg * 2 + 1, 1, False)
            group_b(G - 2, 0, False)
            group_b(G - 1, 1, True)
            norm(3)
            mixture(1)

        @block.vector
        def _(dve):
            links = [0]

            def link(ins):
                ins.then_inc(s_dve, 1)
                links[0] += 1
                dve.wait_ge(s_dve, links[0])

            def norm(phase, src, ready):
                for t in range(T):
                    ready(t)
                    ins = nc.vector.bn_stats(stats[:, t, :], src[:, t, :])
                link(ins)
                for t in range(T):
                    ins = nc.vector.bn_aggr(mv[:, t, :], stats[:, t, :])
                link(ins)
                nc.vector.tensor_scalar(nrm[:, 0, :], mv[:, :, 1], EPS, None, ALU.add).then_inc(s_st, 1)
                dve.wait_ge(s_sq, phase + 1)
                link(nc.vector.reciprocal(nrm[:, 2, :], nrm[:, 1, :]))
                link(nc.vector.tensor_tensor(nrm[:, 3, :], nrm[:, 2, :], nrm[:, 2, :], ALU.mult))
                link(nc.vector.tensor_tensor(nrm[:, 4, :], nrm[:, 3, :], nrm[:, 0, :], ALU.mult))
                link(nc.vector.tensor_scalar(nrm[:, 4, :], nrm[:, 4, :], -0.5, 1.5, ALU.mult, ALU.add))
                link(nc.vector.tensor_tensor(nrm[:, 5, :], nrm[:, 4, :], nrm[:, 2, :], ALU.mult))
                for t in range(T):
                    i = T * phase + t
                    if i >= 2:
                        dve.wait_ge(s_lntr, i - 1)
                    nc.vector.tensor_scalar(xh[:, t % 2, :], src[:, t, :], mv[:, t, 0:1], nrm[:, 5, t:t + 1],
                                            ALU.subtract, ALU.mult).then_inc(s_xh, 1)

            dve.wait_ge(s_cst, 16)
            nc.vector.tensor_copy(identb[:], ident[:]).then_inc(s_idb, 1)
            norm(0, xnat, lambda t: dve.wait_ge(s_x[t], 16))

            def q_parts(n):
                dve.wait_ge(s_q32, 2 * n + 2)
                if n >= 1:
                    dve.wait_ge(s_p2, n)
                    dve.wait_ge(s_p3, n)
                nc.vector.tensor_tensor(r32, q32, parts[:, n % 2, 0, :], ALU.subtract).then_inc(s_r1, 1)
                dve.wait_ge(s_r1, n + 1)
                dve.wait_ge(s_p2, n + 1)
                nc.vector.tensor_tensor(parts[:, n % 2, 2, :], r32, parts[:, n % 2, 1, :], ALU.subtract).then_inc(s_p3, 1)

            q_parts(0)
            q_parts(1)
            dve.wait_ge(s_set, 5)
            for c in range(2):
                dve.wait_ge(s_v, c + 1)
                nc.vector.tensor_tensor(
                    vx[:, 4 * c:4 * c + 4, :, 0:HD],
                    ps[:, 6 + c, :].rearrange("p (t g d) -> p t g d", t=4, g=G),
                    bv.rearrange("p (t g d) -> p t g d", t=1, g=G).broadcast_to([P, 4, G, HD]),
                    ALU.add).then_inc(s_vx, 1)
            for n in range(2, 5):
                q_parts(n)
            for n in range(KC + 3):
                dve.wait_ge(s_wt, n + 1)
                src = ps[:, n % 2, :]
                if n < KC:
                    dst = wbT[:, n, :]
                elif n == KC:
                    dst, src = aT[:], src.rearrange("p (k n) -> p k n", k=KC)
                elif n == KC + 1:
                    dst = bT[:]
                else:
                    dst, src = wrT[:], src[:, 0:KC * NE].rearrange("p (k n) -> p k n", k=KC)
                nc.vector.tensor_copy(dst, src).then_inc(s_we, 1)

            def maxima(u, f, k0, k1):
                for k in range(k0, k1):
                    i = u * MM + k
                    dve.wait_ge(s_mm, i + 1)
                    nc.vector.tensor_reduce(mx[:, f, k // 2, k % 2:k % 2 + 1], ps[:, k % 2, :], AX.X, ALU.max).then_inc(s_mx, 1)

            def negate(u, f, first=False):
                dve.wait_ge(s_mx, u * MM + MM)
                if not first:
                    dve.wait_ge(s_rt, u * 2)
                nc.vector.tensor_reduce(nm[:, 0, :], mx[:, f], AX.X, ALU.max, negate=True).then_inc(s_ch, 1)
                dve.wait_ge(s_ch, u * 5 + 1)
                nc.vector.tensor_copy(mparts[:, :, 0], nm[:, 0, :]).then_inc(s_ch, 1)
                dve.wait_ge(s_ch, u * 5 + 2)
                nc.vector.tensor_tensor(nm[:, 1, :], nm[:, 0, :], mparts[:, :, 0], ALU.subtract).then_inc(s_ch, 1)
                dve.wait_ge(s_ch, u * 5 + 3)
                nc.vector.tensor_copy(mparts[:, :, 1], nm[:, 1, :]).then_inc(s_ch, 1)
                dve.wait_ge(s_ch, u * 5 + 4)
                nc.vector.tensor_tensor(mparts[:, :, 2], nm[:, 1, :], mparts[:, :, 1], ALU.subtract).then_inc(s_ch, 1)

            def normalise(g, f):
                u = g * 2 + f
                dve.wait_ge(s_ot, u + 1)
                o = ps[:, 2, :].rearrange("p (t j w) -> p t j w", t=4, j=R)
                nc.vector.reciprocal(rc, o[:, :, :, HD]).then_inc(s_rec, 1)
                dve.wait_ge(s_rec, u + 1)
                nc.vector.tensor_tensor(
                    oall[:, 4 * f:4 * f + 4, ds(g * (R * HD), R * HD)].rearrange("p t (j d) -> p t j d", j=R),
                    o[:, :, :, 0:HD], rc.unsqueeze(3).broadcast_to([P, 4, R, HD]), ALU.mult).then_inc(s_on, 1)

            def group_a(g, last):
                for f in range(2):
                    u = g * 2 + f
                    if not (last and f == 1):
                        negate(u + 1, 1 - f)
                    if not last:
                        maxima(u + 2, f, 0, 12)
                    if f == 1:
                        normalise(g, 0)
                    if not last:
                        maxima(u + 2, f, 12, MM)
                normalise(g, 1)

            for j in range(5):
                dve.wait_ge(s_stk[j], 16 * len(K_PART))
            maxima(0, 0, 0, MM)
            negate(0, 0, True)
            maxima(1, 1, 0, MM)
            with dve.Fori(0, G - 1) as g:
                group_a(g, False)
            group_a(G - 1, True)

            for i in range(T):
                dve.wait_ge(s_wom, i + 1)
                dve.wait_ge(s_xb, i + 1)
                nc.vector.tensor_tensor(x[:, i, :], x[:, i, :], ps[:, i % 2, :], ALU.add).then_inc(s_xa, 1)
            if stop == 1:
                return
            norm(1, x, lambda t: dve.wait_ge(s_xa, t + 1))

            def route(q, t):
                i = T * q + t
                s = t % 2
                logits = rt8[:, s, 0, :]
                top8 = rt8[:, s, 1, :]
                dve.wait_ge(s_fh, i + 1)
                link(nc.vector.tensor_copy(logits, ps[:, 2 + s, 0:NE]))
                link(nc.vector.max(top8, logits))
                nc.vector.tensor_tensor(rts[:, s, 0:1], top8[:, 1:2], top8[:, 0:1], ALU.subtract).then_inc(s_fd, 1)
                link(nc.vector.max_index(rti[:, s, :], top8, logits))
                link(nc.vector.tensor_copy(rts[:, s, 4:6], rti[:, s, 0:2]))
                dve.wait_ge(s_fe, i + 1)
                link(nc.vector.tensor_scalar(rts[:, s, 2:3], rts[:, s, 1:2], 1.0, None, ALU.add))
                link(nc.vector.reciprocal(rts[:, s, 3:4], rts[:, s, 2:3]))
                link(nc.vector.tensor_scalar(rts[:, s, 2:3], rts[:, s, 3:4], SCALING, None, ALU.mult))
                link(nc.vector.tensor_tensor(rts[:, s, 3:4], rts[:, s, 1:2], rts[:, s, 2:3], ALU.mult))
                link(nc.vector.tensor_scalar(logits, iota8[:], rts[:, s, 4:5], rts[:, s, 2:3], ALU.is_equal, ALU.mult))
                link(nc.vector.tensor_scalar(top8, iota8[:], rts[:, s, 5:6], rts[:, s, 3:4], ALU.is_equal, ALU.mult))
                link(nc.vector.tensor_tensor(logits, logits, top8, ALU.add))
                if i >= 2:
                    dve.wait_ge(s_ft, i - 1)
                nc.vector.tensor_tensor(hid[:, s, :].rearrange("p (e r) -> p e r", e=NE),
                                        ps[:, 2 + s, NE:NE + ER].rearrange("p (e r) -> p e r", e=NE),
                                        logits.unsqueeze(2).broadcast_to([P, NE, RANK]), ALU.mult).then_inc(s_hw, 1)

            def mixture(q, buf):
                def add(t):
                    i = T * q + t
                    dve.wait_ge(s_fy, i + 1)
                    dve.wait_ge(s_xb, T * (q + 1) + t + 1)
                    nc.vector.tensor_tensor(buf[:, t, :], buf[:, t, :], ps[:, 4 + t % 2, :], ALU.add).then_inc(s_fx, 1)

                for t in range(T):
                    route(q, t)
                    if t >= 1:
                        add(t - 1)
                add(T - 1)

            mixture(0, x)
            if stop == 2:
                return
            def dequantise(g, c, par):
                if c < KC:
                    if c == 0:
                        dve.wait_ge(s_wl[0], g * 96 + 96)
                    dst, w, scale = wg[par][:, c, :], stq[:, c, :], scq[:, c, :]
                else:
                    if c == KC:
                        dve.wait_ge(s_wl[1], g * 32 + 32)
                    dst, w, scale = wog[par][:, c - KC, :], sto[:, c - KC, :], sco[:, c - KC, :]
                nc.vector.scalar_tensor_tensor(dst, w.bitcast(I32), -ZERO, scale, ALU.add, ALU.mult).then_inc(s_dq, 1)

            for c in range(2 * KC):
                dequantise(0, c, 0)
            dve.wait_ge(s_nat, 32 * T)
            norm(2, xnat, lambda t: None)

            def rope(v, t):
                dve.wait_ge(s_pj, v + 1)
                src = ps[:, 6:8, :].rearrange("p b n -> p (b n)")[:, 0:BH * P].rearrange("p (h d) -> p h d", h=BH)
                c = cos[:, t:t + 1, :].broadcast_to([P, BH, P])
                s = sin[:, t:t + 1, :].broadcast_to([P, BH, P])
                o1 = rc1.rearrange("p (h d) -> p h d", h=BH)
                o2 = rc2.rearrange("p (h d) -> p h d", h=BH)
                dve.wait_ge(s_vb, v + 1)
                dve.wait_ge(s_qkT, v)
                nc.vector.tensor_tensor(o1, src, c, ALU.mult).then_inc(s_rope, 1)
                for a, b in ((0, P // 2), (P // 2, 0)):
                    nc.vector.tensor_tensor(o2[:, :, a:a + P // 2], src[:, :, b:b + P // 2], s[:, :, a:a + P // 2],
                                            ALU.mult).then_inc(s_rope, 1)

            def maximum(u, h, n):
                dve.wait_ge(s_sc, u * R + h + 1)
                nc.vector.tensor_reduce(mxb[:, h:h + 1], flat(2 * (h % 2), n), AX.X, ALU.max).then_inc(s_mb, 1)
                dve.wait_ge(s_mb, u * R + h + 1)
                nc.vector.tensor_scalar(nmb[:, h:h + 1], mxb[:, h:h + 1], -SC_B, None, ALU.mult).then_inc(s_nb, 1)

            def weigh(u, h, n):
                dve.wait_ge(s_eb, u * R + h + 1)
                nc.vector.reciprocal(rden[:, h:h + 1], den[:, h:h + 1]).then_inc(s_rd, 1)
                dve.wait_ge(s_rd, u * R + h + 1)
                nc.vector.tensor_scalar(pr[:, h, 0:n], pr[:, h, 0:n], rden[:, h:h + 1], None, ALU.mult).then_inc(s_pn, 1)

            def group_b(g, par, last):
                for t in range(T):
                    u = g * T + t
                    n = (t + 1) * P
                    maximum(u, 0, n)
                    for h in range(1, R):
                        maximum(u, h, n)
                        weigh(u, h - 1, n)
                    weigh(u, R - 1, n)
                    if not (last and t == T - 1):
                        rope(u + 1, (t + 1) % T)
                    for kt in range(1, t + 1, 2):
                        dve.wait_ge(s_pt, g * PT_PER_G + before(lambda i: i + 1, t) + kt + 1)
                        nc.vector.tensor_copy(pT[:, kt, :], ps[:, 5, :]).then_inc(s_ptd, 1)
                    dve.wait_ge(s_op, u + 1)
                    nc.vector.tensor_tensor(xnat[:, t, :], xnat[:, t, :], ps[:, 2, :], ALU.add).then_inc(s_xo, 1)
                    if not last:
                        for c in CHUNKS[t]:
                            dequantise(g + 1, c, 1 - par)

            dve.wait_ge(s_tab, 48)
            link(nc.vector.tensor_copy(mask, rc2[:, 0:P]))
            nc.vector.memset(den, 0.0).then_inc(s_xo, 1)
            rope(0, 0)
            with dve.Fori(0, G // 2 - 1) as gg:
                group_b(gg * 2, 0, False)
                group_b(gg * 2 + 1, 1, False)
            group_b(G - 2, 0, False)
            group_b(G - 1, 1, True)
            norm(3, xnat, lambda t: dve.wait_ge(s_xo, (G - 1) * T + t + 2))
            mixture(1, xnat)

        @block.tensor
        def _(pe):
            mm = nc.tensor.matmul

            def norm(phase):
                for t in range(T):
                    i = T * phase + t
                    pe.wait_ge(s_xh, i + 1)
                    if i >= 2:
                        pe.wait_ge(s_xt, i - 1)
                    for k in range(KC):
                        ins = nc.tensor.transpose(ps[:, i % 2, k * P:(k + 1) * P], xh[:, t % 2, k * P:(k + 1) * P], ident[:])
                    ins.then_inc(s_lntr, 1)

            pe.wait_ge(s_cst, 16)
            norm(0)
            pe.wait_ge(s_wqkv, 16 * 6)
            pe.wait_ge(s_xt, T)
            for n, j in enumerate((4, 0, 1, 2, 3)):
                if n >= 2:
                    pe.wait_ge(s_q32, 2 * n - 2)
                for c in range(2):
                    for k in range(KC):
                        lhs = wkv[:, k, 0:P] if j == 4 else wq[:, k, j * P:(j + 1) * P]
                        ins = mm(ps[:, 2 + 2 * (n % 2) + c, :], lhs, xT[:, k, c * HALF:(c + 1) * HALF],
                                 start=(k == 0), stop=(k == KC - 1))
                ins.then_inc(s_qk, 1)
                if n == 1:
                    for t in range(T):
                        for k in range(KC):
                            ins = mm(ps[:, 6 + t // 4, (t % 4) * P:(t % 4 + 1) * P], xT[:, k, t * P:(t + 1) * P],
                                     wkv[:, k, P:2 * P], start=(k == 0), stop=(k == KC - 1))
                        if t % 4 == 3:
                            ins.then_inc(s_v, 1)
            pe.wait_ge(s_raw, 16)
            for n in range(KC + 3):
                if n >= 2:
                    pe.wait_ge(s_we, n - 1)
                if n == KC:
                    pe.wait_ge(s_rawa, 16 * (2 + KC))
                for k in range(KC):
                    if n < KC:
                        src, dst = raw[:, k, n * P:(n + 1) * P], ps[:, n % 2, k * P:(k + 1) * P]
                    elif n == KC:
                        src, dst = raw[:, 0, k * P:(k + 1) * P], ps[:, n % 2, k * P:(k + 1) * P]
                    elif n == KC + 1:
                        src, dst = raw[:, 2, k * P:(k + 1) * P], ps[:, n % 2, k * P:(k + 1) * P]
                    else:
                        src, dst = raw[0:NE, 1, k * P:(k + 1) * P], ps[:, n % 2, k * NE:(k + 1) * NE]
                    ins = nc.tensor.transpose(dst, src, ident[0:src.shape[0], 0:src.shape[0]])
                ins.then_inc(s_wt, 1)

            def maxima(g, f, k0, k1, first=False):
                for k in range(k0, k1):
                    h, qt, kh = k // 8, k // 2 % 4, k % 2
                    if not (first and k < 2):
                        pe.wait_ge(s_mx, (g * 2 + f) * MM + k - 1)
                    mm(ps[:, k % 2, :], qs[0:STACK, ds(g * R + h, 1), f * HALF + qt * P:f * HALF + (qt + 1) * P],
                       ks[0:STACK, ds(g, 1), kh * HALF:(kh + 1) * HALF], start=True, stop=True).then_inc(s_mm, 1)

            def rows(g, f, r, first=False):
                u = g * 2 + f
                if r == 0:
                    pe.wait_ge(s_ch, u * 5 + 5)
                    if f == 0 and not first:
                        pe.wait_ge(s_on, u - 1)
                else:
                    pe.wait_ge(s_rw, u * 2 + 1)
                for i in range(8):
                    ins = nc.tensor.transpose(ps[STACK:STACK + NEG, 2, :].bitcast(BF16)[:, i * P:(i + 1) * P],
                                              mparts[:, 8 * r + i, 0:NEG], identb[:])
                ins.then_inc(s_rt, 1)

            def scores(g, f, kt, r, first=False):
                u = g * 2 + f
                if kt == 0 and r == 0:
                    pe.wait_ge(s_rw, u * 2 + 2)
                if not (first and kt == 0):
                    pe.wait_ge(s_ex, u * (2 * KT) + 2 * kt + r - 1)
                for j in range(2):
                    ins = mm(ps[:, 4 + 2 * r + j, :], ks[0:STACK + NEG, ds(g, 1), kt * P:(kt + 1) * P],
                             qs[0:STACK + NEG, ds(g * R + 2 * r + j, 1), f * HALF:(f + 1) * HALF],
                             start=True, stop=True)
                ins.then_inc(s_sT, 1)

            def context(g, f, kt):
                u = g * 2 + f
                pe.wait_ge(s_ex, u * (2 * KT) + 2 * kt + 2)
                if kt == 0:
                    if f == 1:
                        pe.wait_ge(s_ob, u)
                    else:
                        pe.wait_ge(s_vc, g + 1)
                for j in range(R):
                    ins = mm(ps[VW * j:VW * j + VW, 3, :], vcur[:, kt, :],
                             pbuf[:, 2 * (kt % 2) + j // 2, (j % 2) * HALF:(j % 2 + 1) * HALF],
                             start=(kt == 0), stop=(kt == KT - 1))
                ins.then_inc(s_pv, 1)

            def turn(g, f):
                pe.wait_ge(s_ob, g * 2 + f + 1)
                if f == 1:
                    pe.wait_ge(s_on, g * 2 + 1)
                for i in range(4):
                    ins = nc.tensor.transpose(ps[:, 2, i * P:(i + 1) * P], osb[:, i * P:(i + 1) * P], ident[:])
                ins.then_inc(s_ot, 1)

            def group_a(g, last):
                for f in range(2):
                    end = last and f == 1
                    for kt in range(KT):
                        if f == 1 and kt == 1:
                            turn(g, 0)
                        if kt in (3, 4) and not end:
                            rows(g + f, 1 - f, kt - 3)
                        for r in range(2):
                            if not last:
                                maxima(g + 1, f, 4 * kt + r, 4 * kt + r + 1)
                            if kt < KT - 1:
                                scores(g, f, kt + 1, r)
                            elif not end:
                                scores(g + f, 1 - f, 0, r)
                        if not last:
                            maxima(g + 1, f, 4 * kt + 2, 4 * kt + 3)
                        context(g, f, kt)
                        if not last:
                            maxima(g + 1, f, 4 * kt + 3, 4 * kt + 4)
                turn(g, 1)

            pe.wait_ge(s_we, KC + 3)
            pe.wait_ge(s_idb, 1)
            pe.wait_ge(s_stk[4], 16 * len(K_PART))
            pe.wait_ge(s_stk[0], 16 * len(K_PART))
            maxima(0, 0, 0, MM, True)
            pe.wait_ge(s_q32, 10)
            for r in range(2):
                rows(0, 0, r, True)
            maxima(0, 1, 0, MM)
            for j in range(1, 4):
                pe.wait_ge(s_stk[j], 16 * len(K_PART))
            pe.wait_ge(s_set, 5)
            pe.wait_ge(s_vx, 2)
            for r in range(2):
                scores(0, 0, 0, r, True)
            with pe.Fori(0, G - 1) as g:
                group_a(g, False)
            group_a(G - 1, True)

            pe.wait_ge(s_on, 2 * G)
            pe.wait_ge(s_wo, 16)
            for i in range(T):
                b, f = i // 2, i % 2
                if i >= 2:
                    pe.wait_ge(s_xa, i - 1)
                for c in range(4):
                    ins = mm(ps[:, i % 2, :], oall[:, 4 * f + c, b * P:(b + 1) * P], wo[:, c, :],
                             start=(c == 0), stop=(c == 3))
                ins.then_inc(s_wom, 1)
            if stop == 1:
                return
            norm(1)

            def mixture(q):
                def low_rank(t):
                    i = T * q + t
                    pe.wait_ge(s_hw, i + 1)
                    nc.tensor.transpose(ps[:, 6, 0:P], hid[:, t % 2, :], ident[:]).then_inc(s_ft, 1)
                    pe.wait_ge(s_fc, i + 1)
                    mm(ps[:, 4 + t % 2, :], hidT[:, t % 2, :], bT[:], start=False, stop=True).then_inc(s_fy, 1)

                for t in range(T):
                    i = T * q + t
                    pe.wait_ge(s_xt, T * (2 * q + 1) + t + 1)
                    if i >= 2:
                        pe.wait_ge(s_hw, i - 1)
                    for w, c0, c1 in ((wrT, 0, NE), (aT, NE, NE + ER)):
                        for k in range(KC):
                            ins = mm(ps[:, 2 + t % 2, c0:c1], xT[:, k, t * P:(t + 1) * P], w[:, k, :],
                                     start=(k == 0), stop=(k == KC - 1))
                    ins.then_inc(s_fh, 1)
                    if i >= 2:
                        pe.wait_ge(s_fx, i - 1)
                    for k in range(KC):
                        mm(ps[:, 4 + t % 2, :], xT[:, k, t * P:(t + 1) * P], wbT[:, k, :],
                           start=(k == 0), stop=False)
                    if t >= 1:
                        low_rank(t - 1)
                low_rank(T - 1)

            mixture(0)
            if stop == 2:
                return
            norm(2)

            def project(v, par, t):
                pe.wait_ge(s_rope, v * 3)
                pe.wait_ge(s_vb, v)
                for c0, c1 in ((0, 512), (512, BW)):
                    for k in range(KC):
                        ins = mm(ps[:, 6 + c0 // 512, 0:c1 - c0], xT[:, k, t * P:(t + 1) * P], wg[par][:, k, c0:c1],
                                 start=(k == 0), stop=(k == KC - 1))
                ins.then_inc(s_pj, 1)

            def turn_b(v):
                pe.wait_ge(s_rpa, v + 1)
                for h in range(BH):
                    dst = ps[:, 1, h * P:(h + 1) * P] if h < R else ps[:, 3, 0:P]
                    ins = nc.tensor.transpose(dst, rc1[:, h * P:(h + 1) * P], ident[:])
                ins.then_inc(s_qkT, 1)

            def group_b(g, par, last):
                for t in range(T):
                    u = g * T + t
                    n = (t + 1) * P
                    end = last and t == T - 1
                    pe.wait_ge(s_qke, u * 2 + 2)
                    for h in range(R):
                        if h == 1:
                            pe.wait_ge(s_xo, u + 1)
                        if h >= 2:
                            pe.wait_ge(s_eb, u * R + h - 1)
                        b = 2 * (h % 2)
                        for c in range(0, n, 512):
                            w = min(512, n - c)
                            diag = c + w == n
                            ins = mm(ps[:, b + c // 512, 0:w], qT[:, h, :], kT[:, c:c + w], start=True, stop=not diag)
                            if diag:
                                ins = mm(ps[:, b + c // 512, w - P:w], identb[:], mask, start=False, stop=True)
                        ins.then_inc(s_sc, 1)
                    if not end:
                        if t == T - 1:
                            pe.wait_ge(s_dq, g * 8 + 8 + KC)
                        project(u + 1, par if t < T - 1 else 1 - par, (t + 1) % T)
                    pe.wait_ge(s_pn, u * R + R)
                    for kt in range(t + 2):
                        if kt <= t:
                            for h in range(R):
                                ins = nc.tensor.transpose(ps[:, 4 + kt % 2, h * P:(h + 1) * P],
                                                          pr[:, h, kt * P:(kt + 1) * P], ident[:])
                            ins.then_inc(s_pt, 1)
                        if kt >= 1:
                            k = kt - 1
                            if k % 2 == 0:
                                pe.wait_ge(s_pta, g * ACT_PER_G + before(act_moves, t) + k // 2 + 1)
                            else:
                                pe.wait_ge(s_ptd, g * DVE_PER_G + before(dve_moves, t) + k // 2 + 1)
                            ins = mm(ps[:, 0, :], vB[par][:, k, :], pT[:, k, :], start=(k == 0), stop=(k == t))
                            if k == t:
                                ins.then_inc(s_pvb, 1)
                    if not end:
                        turn_b(u + 1)
                    pe.wait_ge(s_cx, u + 1)
                    if t == 0:
                        pe.wait_ge(s_dq, g * 8 + 8)
                    for h in range(R):
                        ins = mm(ps[:, 2, :], cT[:, h, :], wog[par][:, h, :], start=(h == 0), stop=(h == R - 1))
                    ins.then_inc(s_op, 1)

            pe.wait_ge(s_dq, KC)
            pe.wait_ge(s_xt, 3 * T)
            project(0, 0, 0)
            turn_b(0)
            with pe.Fori(0, G // 2 - 1) as gg:
                group_b(gg * 2, 0, False)
                group_b(gg * 2 + 1, 1, False)
            group_b(G - 2, 0, False)
            group_b(G - 1, 1, True)
            norm(3)
            mixture(1)


_INS = ['L0_attn_a_hidden_state', 'L0_attn_a_wq', 'L0_attn_a_bq', 'L0_attn_a_wk', 'L0_attn_a_bk', 'L0_attn_a_wv',
        'L0_attn_a_bv', 'L0_attn_a_wo', 'L0_attn_a_bo', 'L0_attn_b_scales_q', 'L0_attn_b_scales_k',
        'L0_attn_b_scales_v', 'L0_attn_b_scales_o', 'L0_attn_b_qw_q', 'L0_attn_b_qw_k', 'L0_attn_b_qw_v',
        'L0_attn_b_qw_o', 'L0_ffn_W_base', 'L0_ffn_b_base', 'L0_ffn_W_router', 'L0_ffn_A', 'L0_ffn_B']


def constants():
    f = np.float32
    inv = f(1.0) / np.power(f(10000.0), np.arange(0, P, 2, dtype=f) / f(P))
    ang = np.arange(S, dtype=f)[:, None] * inv
    cos = np.concatenate([np.cos(ang), np.cos(ang)], axis=1).astype(f)
    sin = np.concatenate([-np.sin(ang), np.sin(ang)], axis=1).astype(f)
    mask = np.where(np.tril(np.ones((P, P), bool)), 0.0, -3e38).astype(f)
    return {"ident": np.eye(P, dtype=f), "cos": cos, "sin": sin, "mask": mask}


def kernel(**inputs):
    import concourse.bacc as _bacc
    from concourse.bass_utils import run_bass_kernel_spmd as _run

    nc = _bacc.Bacc("TRN2", target_bir_lowering=False, num_devices=1)
    arrays, args = {}, []
    for name, a in [(n, inputs[n]) for n in _INS] + list(constants().items()):
        a = np.ascontiguousarray(a)
        arrays[f"in_{name}_dram"] = a
        args.append(nc.dram_tensor(f"in_{name}_dram", a.shape, mybir.dt.from_np(a.dtype), kind="ExternalInput").ap())
    args.append(nc.dram_tensor("out_0_dram", (1, S, D), F32, kind="ExternalOutput").ap())
    build(nc, *args)
    r = _run(nc, [arrays], core_ids=[0])
    return r.results[0]["out_0_dram"]
```

```python
from contextlib import ExitStack

import numpy as np

import concourse.bass as bass
from concourse import mybir

P = 128
S = 1024
D = 512
T = S // P
KC = D // P
HALF = S // 2

NH = 32
G = 8
R = NH // G
HD = D // NH
K_PART = (0, 0, 1, 0, 1, 2)
Q_PART = (0, 1, 0, 2, 1, 0)
STACK = HD * len(K_PART)
NEG = 3
KT = S // P
MM = R * (HALF // P) * 2
PTS = 4
VW = 32

BW = R * P + 2 * P
BH = R + 1
SC_B = float(P) ** -0.5
ZERO = 8.0

NE = 8
RANK = 16
ER = NE * RANK
SCALING = 2.0
EPS = 1e-5

F32 = mybir.dt.float32
F32R = mybir.dt.float32r
BF16 = mybir.dt.bfloat16
I32 = mybir.dt.int32
U32 = mybir.dt.uint32
ALU = mybir.AluOpType
ACT = mybir.ActivationFunctionType
AX = mybir.AxisListType
ds = bass.ds


def build(nc, x_d, wq_d, bq_d, wk_d, bk_d, wv_d, bv_d, wo_d, bo_d,
          sq_d, sk_d, sv_d, so_d, qq_d, qk_d, qv_d, qo_d,
          wb_d, bb_d, wr_d, a_d, b_d, ident_d, cos_d, sin_d, mask_d, out_d):
    x_nat = x_d.rearrange("o (t p) d -> (o t) p d", p=P)
    x_il = x_d.rearrange("o (b p f) d -> p (o b) f d", p=P, f=2)
    out_nat = out_d.rearrange("o (t p) d -> (o t) p d", p=P)

    with ExitStack() as ctx:
        def sb(name, shape, dt=F32):
            return ctx.enter_context(nc.sbuf_tensor(name, shape, dt))

        def sem(name):
            return ctx.enter_context(nc.semaphore(name))

        x = sb("x", [P, T, D])
        xnat = sb("xnat", [P, T, D])
        ident = sb("ident", [P, P])
        identb = sb("identb", [P, P], BF16)
        wbT = sb("wbT", [P, KC, D])
        wrT = sb("wrT", [P, KC, NE])
        aT = sb("aT", [P, KC, ER])
        bT = sb("bT", [P, D])
        bb = sb("bb", [P, D])
        xh = sb("xh", [P, 2, D])
        stats = sb("stats", [P, T, 6])
        mv = sb("mv", [P, T, 2])
        nrm = sb("nrm", [P, 6, T])
        hid = sb("hid", [P, 2, ER])
        hidT = sb("hidT", [P, 2, P])
        iota8 = sb("iota8", [P, NE])
        iota8i = sb("iota8i", [P, NE], I32)
        rt8 = sb("rt8", [P, 2, 2, NE])
        rti = sb("rti", [P, 2, NE], U32)
        rts = sb("rts", [P, 2, 8])

        def scoped(mem, name, shape, dt=F32):
            return mem.enter_context(nc.sbuf_tensor(name, shape, dt))

        with ExitStack() as mem:
            xT = scoped(mem, "xT", [P, KC, S])
            proj = scoped(mem, "proj", [P, 4 * S])
            wq = proj[:, 0:KC * D].rearrange("p (k n) -> p k n", k=KC)
            wkv = proj[:, KC * D:KC * (D + 2 * P)].rearrange("p (k n) -> p k n", k=KC)
            q32 = proj[:, 3 * S:4 * S]
            pbuf = proj[:].rearrange("p (b n) -> p b n", b=4)
            pieces = scoped(mem, "pieces", [P, 4 * S])
            r32 = pieces[:, 0:S]
            parts = pieces[:, S:4 * S].bitcast(BF16).rearrange("p (b c n) -> p b c n", b=2, c=3)
            oall = pieces[:].rearrange("p (t n) -> p t n", t=T)
            qs = scoped(mem, "qs", [P, NH, S], BF16)
            ks = scoped(mem, "ks", [P, G, S], BF16)
            vx = scoped(mem, "vx", [P, KT, G, VW])
            vcur = scoped(mem, "vcur", [P, KT, VW])
            osb = scoped(mem, "osb", [P, HALF])
            mx = scoped(mem, "mx", [P, 2, MM // 2, 2])
            nm = scoped(mem, "nm", [P, 2, MM // 2])
            mparts = scoped(mem, "mparts", [P, MM // 2, 4], BF16)
            rc = scoped(mem, "rc", [P, 4, R])
            bqk = scoped(mem, "bqk", [P, 8])
            bv = scoped(mem, "bv", [P, P])
            bo = scoped(mem, "bo", [P, D])
        wo = xT[:, 0:2, :].rearrange("p a (b n) -> p (a b) n", b=2)
        raw = x[:, 0:KC, :]

        with ExitStack() as mem:
            pTh, pTl = (scoped(mem, f"pT{c}", [P, PTS, R * P], F32R) for c in "hl")
            xTh, xTl = (scoped(mem, f"xT{c}", [P, KC, S], F32R) for c in "hl")
            wh, wl = (scoped(mem, f"w{c}", [P, KC, BW], F32R) for c in "hl")
            woh, wol = (scoped(mem, f"wo{c}", [P, R, D], F32R) for c in "hl")
            stq = scoped(mem, "stq", [P, KC, BW])
            sto = scoped(mem, "sto", [P, R, D])
            scale = scoped(mem, "scale", [P, 2, BW])
            qTh, qTl = (scoped(mem, f"qT{c}", [P, R, P], F32R) for c in "hl")
            kTh, kTl = (scoped(mem, f"kT{c}", [P, S], F32R) for c in "hl")
            vh, vl = (scoped(mem, f"v{c}", [P, T + 1, P], F32R) for c in "hl")
            cTh, cTl = (scoped(mem, f"cT{c}", [P, R, P], F32R) for c in "hl")
            rc1 = scoped(mem, "rc1", [P, BH * P])
            rc2 = scoped(mem, "rc2", [P, BH * P])
            cos = scoped(mem, "cosines", [P, T, P])
            sin = scoped(mem, "sines", [P, T, P])
            mask = scoped(mem, "mask", [P, P], BF16)
            nmb = scoped(mem, "nmb", [P, R])
            den = scoped(mem, "den", [P, R])
            rden = scoped(mem, "rden", [P, R])
        pr = x[:].rearrange("p (h b) n -> p h (b n)", h=R)

        def v_slot(t, par):
            return t if t else T * par

        ps = ctx.enter_context(nc.psum_tensor("ps", [P, 8, 512], F32))
        scratch = nc.dram_tensor("scratch", (5, 3, P, S), BF16, kind="Internal").ap()

        s_x = [sem(f"s_x{t}") for t in range(T)]
        s_wqkv = sem("s_wqkv")
        s_xr = sem("s_xr")
        s_wo = sem("s_wo")
        s_cst = sem("s_cst")
        s_raw = sem("s_raw")
        s_rawa = sem("s_rawa")
        s_idb = sem("s_idb")
        s_set = sem("s_set")
        s_st = sem("s_stats")
        s_sq = sem("s_sqrt")
        s_xh = sem("s_xh")
        s_lntr = sem("s_lntr")
        s_xt = sem("s_xt")
        s_qk = sem("s_qk")
        s_q32 = sem("s_q32")
        s_r1 = sem("s_r1")
        s_p2 = sem("s_p2")
        s_p3 = sem("s_p3")
        s_stk = [sem(f"s_stk{j}") for j in range(5)]
        s_scr = [sem(f"s_scr{n}") for n in range(5)]
        s_v = sem("s_v")
        s_vx = sem("s_vx")
        s_wt = sem("s_wt")
        s_we = sem("s_we")
        s_mm = sem("s_mm")
        s_mx = sem("s_mx")
        s_ch = sem("s_ch")
        s_rt = sem("s_rt")
        s_rw = sem("s_rw")
        s_sT = sem("s_sT")
        s_ex = sem("s_ex")
        s_vc = sem("s_vc")
        s_pv = sem("s_pv")
        s_ob = sem("s_ob")
        s_ot = sem("s_ot")
        s_on = sem("s_on")
        s_rec = sem("s_rec")
        s_wom = sem("s_wom")
        s_xa = sem("s_xa")
        s_xb = sem("s_xb")
        s_fh = sem("s_fh")
        s_fd = sem("s_fd")
        s_fe = sem("s_fe")
        s_hw = sem("s_hw")
        s_ft = sem("s_ft")
        s_fc = sem("s_fc")
        s_fy = sem("s_fy")
        s_fx = sem("s_fx")
        s_dve = sem("s_dve")
        s_nat = [sem(f"s_nat{b}") for b in range(T // 2)]
        s_out = sem("s_out")
        s_tab = sem("s_tab")
        s_wl = [sem(f"s_wl{c}") for c in range(KC + R)]
        s_wh = sem("s_wh")
        s_wlp = sem("s_wlp")
        s_wld = sem("s_wld")
        s_xl = sem("s_xl")
        s_dq = sem("s_dq")
        s_pj = sem("s_pj")
        s_rope = sem("s_rope")
        s_rpa = sem("s_rpa")
        s_vb = sem("s_vb")
        s_qkT = sem("s_qkT")
        s_qke = sem("s_qke")
        s_sc = sem("s_sc")
        s_pd = sem("s_pd")
        s_nb = sem("s_nb")
        s_eb = sem("s_eb")
        s_rd = sem("s_rd")
        s_pn = sem("s_pn")
        s_pt = sem("s_pt")
        s_ph = sem("s_ph")
        s_pl = sem("s_pl")
        s_pvb = sem("s_pvb")
        s_ch_b = sem("s_ctx_hi")
        s_cx = sem("s_ctx_lo")
        s_ql = sem("s_qk_lo")
        s_op = sem("s_op")
        s_xo = sem("s_xo")

        def flat(bank, n):
            return ps[:, bank:bank + 2, :].rearrange("p b n -> p (b n)")[:, 0:n]

        CHUNKS = {0: (), 1: (), 2: (), 3: (0,), 4: (1, 2), 5: (3, 4), 6: (5, 6), 7: (7,)}

        PT_PER_G = sum(t + 1 for t in range(T))
        PT_BANK = (5, 1, 3, 4)
        HALVED = (1, 2)
        SHORT = 4
        LATE_VALUES = 3
        TURN = 4

        def key_tile(g, t, kt):
            return g * PT_PER_G + t * (t + 1) // 2 + kt

        def after(g, par, t):
            return (g, par, t + 1) if t < T - 1 else (g + 1, 1 - par, 0)

        block = ctx.enter_context(nc.Block())


        @block.sync
        def _(sp):
            for t in range(T):
                sp.dma_start(xnat[:, t, :], x_nat[t]).then_inc(s_x[t], 16)
                if t == 0:
                    sp.dma_start(ident[:], ident_d).then_inc(s_cst, 16)
            sp.dma_start(wkv[:, :, 0:P], wk_d.rearrange("(k p) n -> p k n", p=P)).then_inc(s_wqkv, 16)
            sp.dma_start(bqk[:, 0:4], bq_d.rearrange("(j p) -> p j", p=P), allow_slow_non_contiguous=True).then_inc(s_wqkv, 16)
            sp.dma_start(bqk[:, 4:5], bk_d.rearrange("(j p) -> p j", p=P), allow_slow_non_contiguous=True).then_inc(s_wqkv, 16)
            sp.dma_start(wq, wq_d.rearrange("(k p) n -> p k n", p=P)).then_inc(s_wqkv, 16)
            sp.dma_start(wkv[:, :, P:], wv_d.rearrange("(k p) n -> p k n", p=P)).then_inc(s_wqkv, 16)
            sp.dma_start(bv[:], bv_d.partition_broadcast(P)).then_inc(s_wqkv, 16)
            sp.dma_start(raw, wb_d.rearrange("(t p) d -> p t d", p=P)).then_inc(s_raw, 16)
            for n, j in enumerate((4, 0, 1, 2, 3)):
                sp.wait_ge(s_p2, n + 1)
                sp.wait_ge(s_p3, n + 1)
                sp.dma_start(scratch[n].rearrange("c p n -> p c n"), parts[:, n % 2]).then_inc(s_scr[n], 16)
                sp.wait_ge(s_scr[n], 16)
                for b in range(len(K_PART)):
                    rows = slice(HD * b, HD * b + HD)
                    dst, part = (ks[rows], K_PART[b]) if j == 4 else (qs[rows, 8 * j:8 * j + 8, :], Q_PART[b])
                    sp.dma_start(dst, scratch[n, part].rearrange("(h d) n -> d h n", d=HD)).then_inc(s_stk[j], 16)
            sp.wait_ge(s_wt, KC)
            sp.dma_start(raw[:, 0, :], a_d.rearrange("e r d -> (e r) d")).then_inc(s_rawa, 16)
            sp.dma_start(raw[0:NE, 1, :], wr_d).then_inc(s_rawa, 16)
            for t in range(KC):
                sp.dma_start(raw[:, 2, t * ER:(t + 1) * ER].rearrange("p (e r) -> p e r", r=RANK),
                             b_d[:, t * P:(t + 1) * P, :].rearrange("e o r -> o e r")).then_inc(s_rawa, 16)
            sp.wait_ge(s_qk, 5)
            sp.wait_ge(s_v, 2)
            sp.dma_start(wo, wo_d.rearrange("(k p) n -> p k n", p=P)).then_inc(s_wo, 16)
            sp.wait_ge(s_wt, KC + 3)
            for b in range(T // 2):
                sp.dma_start(x[:, 2 * b:2 * b + 2, :], x_il[:, b]).then_inc(s_xr, 16)
            sp.dma_start(bo[:], bo_d.partition_broadcast(P)).then_inc(s_xr, 16)
            sp.dma_start(bb[:], bb_d.partition_broadcast(P)).then_inc(s_xr, 16)

            sp.wait_ge(s_xa, T)
            sp.dma_start(cos[:], cos_d.rearrange("(t p) d -> p t d", p=P)).then_inc(s_tab, 16)
            sp.dma_start(sin[:], sin_d.rearrange("(t p) d -> p t d", p=P)).then_inc(s_tab, 16)
            sp.dma_start(rc2[:, 0:P], mask_d).then_inc(s_tab, 16)

            def load_chunk(g, c):
                if c < KC:
                    for c0, w, w_d, s_d in ((0, R * P, qq_d, sq_d), (R * P, P, qk_d, sk_d), (R * P + P, P, qv_d, sv_d)):
                        sp.dma_start(stq[:, c, c0:c0 + w].bitcast(I32),
                                     w_d[c * P:(c + 1) * P, ds(g * w, w)]).then_inc(s_wl[c], 16)
                        sp.dma_start(scale[:, c % 2, c0:c0 + w],
                                     s_d[c:c + 1, ds(g * w, w)].rearrange("o n -> (o n)").partition_broadcast(P)).then_inc(s_wl[c], 16)
                else:
                    h = c - KC
                    sp.dma_start(sto[:, h, :].bitcast(I32), qo_d[ds(g * (R * P) + h * P, P), :]).then_inc(s_wl[c], 16)
                    sp.dma_start(scale[:, c % 2, 0:D],
                                 so_d[ds(g * R + h, 1), :].rearrange("o n -> (o n)").partition_broadcast(P)).then_inc(s_wl[c], 16)

            load_chunk(0, 0)
            load_chunk(0, 1)
            for t in range(T):
                if t < T - 2:
                    sp.wait_ge(s_dq, t + 1)
                    load_chunk(0, t + 2)
                if t % 2:
                    sp.wait_ge(s_fx, t + 1)
                    for n in (t - 1, t):
                        for f in range(2):
                            sp.dma_start(xnat[f:P:2, n, :],
                                         x[HALF // 8 * (n % 2):HALF // 8 * (n % 2) + HALF // 8, 2 * (t // 2) + f, :]
                                         ).then_inc(s_nat[t // 2], 16)
            with sp.Fori(0, G - 1) as g:
                for c in range(KC + R):
                    if c < 2:
                        sp.wait_ge(s_wld, g * R + 1)
                    else:
                        sp.wait_ge(s_dq, g * 8 + 8 + c - 1)
                    load_chunk(g + 1, c)
            for t in range(T):
                sp.wait_ge(s_fx, T + t + 1)
                sp.dma_start(out_nat[t], xnat[:, t, :]).then_inc(s_out, 16)
            sp.wait_ge(s_out, 16 * T)

        @block.gpsimd
        def _(pool):
            pool.iota(iota8i[:], pattern=[[1, NE]], base=0, channel_multiplier=0).then_inc(s_set, 1)
            pool.memset(vx[:], 0.0).then_inc(s_set, 1)
            pool.wait_ge(s_set, 2)
            pool.memset(ks[STACK:STACK + NEG], 1.0).then_inc(s_set, 1)
            pool.wait_ge(s_set, 3)
            pool.memset(vx[:, :, :, HD:HD + 1], 1.0).then_inc(s_set, 1)
            pool.tensor_copy(iota8[:], iota8i[:]).then_inc(s_set, 1)
            for n in range(5):
                pool.wait_ge(s_r1, n + 1)
                pool.tensor_copy(parts[:, n % 2, 1, :], r32).then_inc(s_p2, 1)
            pool.wait_ge(s_xr, 16 * 6)
            for t in range(T):
                pool.tensor_tensor(x[:, t, :], x[:, t, :], bo[:], ALU.add).then_inc(s_xb, 1)
            pool.wait_ge(s_vx, 2)
            pool.tensor_copy(vcur[:], vx[:, :, 0, :]).then_inc(s_vc, 1)
            with pool.Fori(1, G) as g:
                pool.wait_ge(s_pv, g * (2 * KT))
                pool.tensor_copy(vcur[:], vx[:, :, ds(g, 1), :].rearrange("p t g w -> p t (g w)")).then_inc(s_vc, 1)
            def add_base_bias(buf, phase):
                for t in range(T):
                    pool.wait_ge(s_xh, T * phase + t + 1)
                    pool.tensor_tensor(buf[:, t, :], buf[:, t, :], bb[:], ALU.add).then_inc(s_xb, 1)

            add_base_bias(x, 1)
            def rope_add(v):
                pool.wait_ge(s_rope, v * 4 + 4)
                pool.tensor_tensor(rc1[:], rc1[:], rc2[:], ALU.add).then_inc(s_rpa, 1)

            def low_parts(g):
                for c in range(KC):
                    pool.wait_ge(s_wh, g * 8 + c + 1)
                    pool.tensor_tensor(wl[:, c, :], stq[:, c, :], wh[:, c, :].bitcast(F32), ALU.subtract).then_inc(s_wlp, 1)

            def group(g, last):
                for t in range(T - 1 if last else T):
                    rope_add(g * T + t + 1)
                    if t == T - 2 and not last:
                        low_parts(g + 1)

            low_parts(0)
            rope_add(0)
            with pool.Fori(0, G - 1) as g:
                group(g, False)
            group(G - 1, True)
            add_base_bias(xnat, 3)

        @block.scalar
        def _(act):
            def norm(phase, dst=None):
                dst = xT if dst is None else dst
                act.wait_ge(s_st, phase + 1)
                nc.scalar.activation(nrm[:, 1, :], nrm[:, 0, :], ACT.Sqrt).then_inc(s_sq, 1)
                for t in range(T):
                    i = T * phase + t
                    act.wait_ge(s_lntr, i + 1)
                    nc.scalar.activation(dst[:, :, t * P:(t + 1) * P],
                                         ps[:, i % 2, :].rearrange("p (k n) -> p k n", k=KC), ACT.Copy).then_inc(s_xt, 1)

            norm(0)
            act.wait_ge(s_wqkv, 16 * 6)
            for n, j in enumerate((4, 0, 1, 2, 3)):
                b = 2 + 2 * (n % 2)
                act.wait_ge(s_qk, n + 1)
                if n >= 1:
                    act.wait_ge(s_r1, n)
                nc.scalar.activation(q32.rearrange("p (b n) -> p b n", b=2), ps[:, b:b + 2, :], ACT.Identity,
                                     bias=bqk[:, j:j + 1]).then_inc(s_q32, 1)
                if n >= 2:
                    act.wait_ge(s_scr[n - 2], 16)
                nc.scalar.activation(parts[:, n % 2, 0, :].rearrange("p (b n) -> p b n", b=2), ps[:, b:b + 2, :],
                                     ACT.Identity, bias=bqk[:, j:j + 1]).then_inc(s_q32, 1)

            def row_copy(v, r):
                g, f = v
                n = (g * 2 + f) * 2 + r
                act.wait_ge(s_rt, n + 1)
                nc.scalar.activation(
                    qs[STACK:STACK + NEG, ds(g * R + 2 * r, 2), f * HALF:(f + 1) * HALF],
                    ps[STACK:STACK + NEG, 2, :].bitcast(BF16).rearrange("p (h n) -> p h n", h=2),
                    ACT.Copy).then_inc(s_rw, 1)

            def o_copy(u):
                act.wait_ge(s_pv, u * KT + KT)
                nc.scalar.activation(osb[:], ps[:, 3, :], ACT.Copy).then_inc(s_ob, 1)

            def exps(g, last):
                for f in range(2):
                    u = g * 2 + f
                    for e in range(2 * KT):
                        act.wait_ge(s_sT, u * (2 * KT) + e + 1)
                        if f == 1 or e >= 4:
                            act.wait_ge(s_pv, u * KT + e // 2 - 1)
                        b = 4 + 2 * (e % 2)
                        nc.scalar.activation(pbuf[:, e % 4, :].rearrange("p (b n) -> p b n", b=2), ps[:, b:b + 2, :],
                                             ACT.Exp, scale=float(HD) ** -0.5).then_inc(s_ex, 1)
                        if f == 1 and e == 1:
                            o_copy(g * 2)
                        if e in (8, 10) and not (last and f == 1):
                            row_copy((g + f, 1 - f), (e - 8) // 2)
                o_copy(g * 2 + 1)

            for r in range(2):
                row_copy((0, 0), r)
            with act.Fori(0, G - 1) as g:
                exps(g, False)
            exps(G - 1, True)
            norm(1)

            def high_parts(g, c):
                act.wait_ge(s_dq, g * 8 + c + 1)
                if c < KC:
                    nc.scalar.activation(wh[:, c, :], stq[:, c, :], ACT.Copy).then_inc(s_wh, 1)
                else:
                    nc.scalar.activation(woh[:, c - KC, :], sto[:, c - KC, :], ACT.Copy).then_inc(s_wh, 1)

            def mixture(q):
                for t in range(T):
                    i = T * q + t
                    act.wait_ge(s_fd, i + 1)
                    nc.scalar.activation(rts[:, t % 2, 1:2], rts[:, t % 2, 0:1], ACT.Exp).then_inc(s_fe, 1)
                    act.wait_ge(s_ft, i + 1)
                    nc.scalar.activation(hidT[:, t % 2, :], ps[:, 6, 0:P], ACT.Copy).then_inc(s_fc, 1)
                    if q == 0 and t < KC:
                        high_parts(0, t)

            mixture(0)
            norm(2, xTh)

            def values(v, par, t):
                act.wait_ge(s_pj, v + 1)
                nc.scalar.activation(vh[:, v_slot(t, par), :], ps[:, 7, P:2 * P], ACT.Copy).then_inc(s_vb, 1)

            def turned(v, t):
                act.wait_ge(s_qkT, v + 1)
                nc.scalar.activation(qTh[:].rearrange("p h n -> p (h n)"), ps[:, 6, :], ACT.Copy, scale=SC_B).then_inc(s_qke, 1)
                nc.scalar.activation(kTh[:, t * P:(t + 1) * P], ps[:, 7, 0:P], ACT.Copy).then_inc(s_qke, 1)

            def front(g, par, t, last):
                u = g * T + t
                n = (t + 1) * P

                def exponentials(h):
                    act.wait_ge(s_nb, u * R + h + 1)
                    nc.scalar.activation(pr[:, h, 0:n], flat(2 * (h % 2), n), ACT.Exp, bias=nmb[:, h:h + 1],
                                         accum_out=den[:, h:h + 1]).then_inc(s_eb, 1)

                def weigh(h):
                    act.wait_ge(s_rd, u * R + h + 1)
                    nc.scalar.activation(pr[:, h, 0:n], pr[:, h, 0:n], ACT.Copy, scale=rden[:, h:h + 1]).then_inc(s_pn, 1)

                exponentials(0)
                exponentials(1)
                weigh(0)
                if t == 1:
                    high_parts(g, 6)
                    high_parts(g, 7)
                end = last and t == T - 1
                _, p2, t2 = after(g, par, t)
                if t < LATE_VALUES and not end:
                    values(u + 1, p2, t2)
                exponentials(2)
                exponentials(3)
                if t >= LATE_VALUES and not end:
                    values(u + 1, p2, t2)
                weigh(2)
                if t == T - 2 and not last:
                    high_parts(g + 1, 0)

            def back(g, par, t, last):
                u = g * T + t
                for kt in range(t + 1):
                    act.wait_ge(s_pt, key_tile(g, t, kt) + 1)
                    if kt >= PTS:
                        act.wait_ge(s_pvb, key_tile(g, t, kt - PTS) + 1)
                    nc.scalar.activation(pTh[:, kt % PTS, :], ps[:, PT_BANK[kt % PTS], :], ACT.Copy).then_inc(s_ph, 1)
                    if kt == min(t, TURN) and not (last and t == T - 1):
                        turned(u + 1, (t + 1) % T)
                    if t == T - 2 and not last and kt in (2, 4):
                        high_parts(g + 1, kt // 2)
                if t == T - 2 and not last:
                    high_parts(g + 1, 3)
                act.wait_ge(s_pvb, key_tile(g, t, t) + 1)
                nc.scalar.activation(cTh[:].rearrange("p h n -> p (h n)"), ps[:, 2, :], ACT.Copy).then_inc(s_ch_b, 1)
                if t == 0:
                    high_parts(g, 4)
                    high_parts(g, 5)

            values(0, 0, 0)
            turned(0, 0)
            front(0, 0, 0, False)
            with act.Fori(0, G // 2 - 1) as gg:
                for par in range(2):
                    for t in range(T):
                        back(gg * 2 + par, par, t, False)
                        front(*after(gg * 2 + par, par, t), False)
            for n in range(2 * T):
                g, par, t = G - 2 + n // T, n // T, n % T
                back(g, par, t, g == G - 1)
                if n < 2 * T - 1:
                    front(*after(g, par, t), g == G - 1 or t == T - 1)
            norm(3)
            mixture(1)

        @block.vector
        def _(dve):
            links = [0]

            def link(ins):
                ins.then_inc(s_dve, 1)
                links[0] += 1
                dve.wait_ge(s_dve, links[0])

            def norm(phase, src, ready, low=None):
                for t in range(T):
                    ready(t)
                    ins = nc.vector.bn_stats(stats[:, t, :], src[:, t, :])
                link(ins)
                for t in range(T):
                    ins = nc.vector.bn_aggr(mv[:, t, :], stats[:, t, :])
                link(ins)
                nc.vector.tensor_scalar(nrm[:, 0, :], mv[:, :, 1], EPS, None, ALU.add).then_inc(s_st, 1)
                dve.wait_ge(s_sq, phase + 1)
                link(nc.vector.reciprocal(nrm[:, 2, :], nrm[:, 1, :]))
                link(nc.vector.tensor_tensor(nrm[:, 3, :], nrm[:, 2, :], nrm[:, 2, :], ALU.mult))
                link(nc.vector.tensor_tensor(nrm[:, 4, :], nrm[:, 3, :], nrm[:, 0, :], ALU.mult))
                link(nc.vector.tensor_scalar(nrm[:, 4, :], nrm[:, 4, :], -0.5, 1.5, ALU.mult, ALU.add))
                link(nc.vector.tensor_tensor(nrm[:, 5, :], nrm[:, 4, :], nrm[:, 2, :], ALU.mult))
                for t in range(T):
                    i = T * phase + t
                    if i >= 2:
                        dve.wait_ge(s_lntr, i - 1)
                    nc.vector.tensor_scalar(xh[:, t % 2, :], src[:, t, :], mv[:, t, 0:1], nrm[:, 5, t:t + 1],
                                            ALU.subtract, ALU.mult).then_inc(s_xh, 1)
                    if low is not None and t >= 1:
                        low(t - 1)
                if low is not None:
                    low(T - 1)

            dve.wait_ge(s_cst, 16)
            nc.vector.tensor_copy(identb[:], ident[:]).then_inc(s_idb, 1)
            norm(0, xnat, lambda t: dve.wait_ge(s_x[t], 16))

            def q_parts(n):
                dve.wait_ge(s_q32, 2 * n + 2)
                if n >= 1:
                    dve.wait_ge(s_p2, n)
                    dve.wait_ge(s_p3, n)
                nc.vector.tensor_tensor(r32, q32, parts[:, n % 2, 0, :], ALU.subtract).then_inc(s_r1, 1)
                dve.wait_ge(s_r1, n + 1)
                dve.wait_ge(s_p2, n + 1)
                nc.vector.tensor_tensor(parts[:, n % 2, 2, :], r32, parts[:, n % 2, 1, :], ALU.subtract).then_inc(s_p3, 1)

            q_parts(0)
            q_parts(1)
            dve.wait_ge(s_set, 5)
            for c in range(2):
                dve.wait_ge(s_v, c + 1)
                nc.vector.tensor_tensor(
                    vx[:, 4 * c:4 * c + 4, :, 0:HD],
                    ps[:, 6 + c, :].rearrange("p (t g d) -> p t g d", t=4, g=G),
                    bv[:].rearrange("p (t g d) -> p t g d", t=1, g=G).broadcast_to([P, 4, G, HD]),
                    ALU.add).then_inc(s_vx, 1)
            for n in range(2, 5):
                q_parts(n)
            for n in range(KC + 3):
                dve.wait_ge(s_wt, n + 1)
                src = ps[:, n % 2, :]
                if n < KC:
                    dst = wbT[:, n, :]
                elif n == KC:
                    dst, src = aT[:], src.rearrange("p (k n) -> p k n", k=KC)
                elif n == KC + 1:
                    dst = bT[:]
                else:
                    dst, src = wrT[:], src[:, 0:KC * NE].rearrange("p (k n) -> p k n", k=KC)
                nc.vector.tensor_copy(dst, src).then_inc(s_we, 1)

            def maxima(u, f, k0, k1):
                for k in range(k0, k1):
                    i = u * MM + k
                    dve.wait_ge(s_mm, i + 1)
                    nc.vector.tensor_reduce(mx[:, f, k // 2, k % 2:k % 2 + 1], ps[:, k % 2, :], AX.X, ALU.max).then_inc(s_mx, 1)

            def negate(u, f, first=False):
                dve.wait_ge(s_mx, u * MM + MM)
                if not first:
                    dve.wait_ge(s_rt, u * 2)
                nc.vector.tensor_reduce(nm[:, 0, :], mx[:, f], AX.X, ALU.max, negate=True).then_inc(s_ch, 1)
                dve.wait_ge(s_ch, u * 5 + 1)
                nc.vector.tensor_copy(mparts[:, :, 0], nm[:, 0, :]).then_inc(s_ch, 1)
                dve.wait_ge(s_ch, u * 5 + 2)
                nc.vector.tensor_tensor(nm[:, 1, :], nm[:, 0, :], mparts[:, :, 0], ALU.subtract).then_inc(s_ch, 1)
                dve.wait_ge(s_ch, u * 5 + 3)
                nc.vector.tensor_copy(mparts[:, :, 1], nm[:, 1, :]).then_inc(s_ch, 1)
                dve.wait_ge(s_ch, u * 5 + 4)
                nc.vector.tensor_tensor(mparts[:, :, 2], nm[:, 1, :], mparts[:, :, 1], ALU.subtract).then_inc(s_ch, 1)

            def normalise(g, f):
                u = g * 2 + f
                dve.wait_ge(s_ot, u + 1)
                o = ps[:, 2, :].rearrange("p (t j w) -> p t j w", t=4, j=R)
                nc.vector.reciprocal(rc[:], o[:, :, :, HD]).then_inc(s_rec, 1)
                dve.wait_ge(s_rec, u + 1)
                nc.vector.tensor_tensor(
                    oall[:, 4 * f:4 * f + 4, ds(g * (R * HD), R * HD)].rearrange("p t (j d) -> p t j d", j=R),
                    o[:, :, :, 0:HD], rc[:].unsqueeze(3).broadcast_to([P, 4, R, HD]), ALU.mult).then_inc(s_on, 1)

            def group_a(g, last):
                for f in range(2):
                    u = g * 2 + f
                    if not (last and f == 1):
                        negate(u + 1, 1 - f)
                    if not last:
                        maxima(u + 2, f, 0, 12)
                    if f == 1:
                        normalise(g, 0)
                    if not last:
                        maxima(u + 2, f, 12, MM)
                normalise(g, 1)

            for j in range(5):
                dve.wait_ge(s_stk[j], 16 * len(K_PART))
            maxima(0, 0, 0, MM)
            negate(0, 0, True)
            maxima(1, 1, 0, MM)
            with dve.Fori(0, G - 1) as g:
                group_a(g, False)
            group_a(G - 1, True)

            for i in range(T):
                dve.wait_ge(s_wom, i + 1)
                dve.wait_ge(s_xb, i + 1)
                nc.vector.tensor_tensor(x[:, i, :], x[:, i, :], ps[:, i % 2, :], ALU.add).then_inc(s_xa, 1)
            norm(1, x, lambda t: dve.wait_ge(s_xa, t + 1))

            def route(q, t):
                i = T * q + t
                s = t % 2
                logits = rt8[:, s, 0, :]
                top8 = rt8[:, s, 1, :]
                dve.wait_ge(s_fh, i + 1)
                link(nc.vector.tensor_copy(logits, ps[:, 2 + s, 0:NE]))
                link(nc.vector.max(top8, logits))
                nc.vector.tensor_tensor(rts[:, s, 0:1], top8[:, 1:2], top8[:, 0:1], ALU.subtract).then_inc(s_fd, 1)
                link(nc.vector.max_index(rti[:, s, :], top8, logits))
                link(nc.vector.tensor_copy(rts[:, s, 4:6], rti[:, s, 0:2]))
                dve.wait_ge(s_fe, i + 1)
                link(nc.vector.tensor_scalar(rts[:, s, 2:3], rts[:, s, 1:2], 1.0, None, ALU.add))
                link(nc.vector.reciprocal(rts[:, s, 3:4], rts[:, s, 2:3]))
                link(nc.vector.tensor_scalar(rts[:, s, 2:3], rts[:, s, 3:4], SCALING, None, ALU.mult))
                link(nc.vector.tensor_tensor(rts[:, s, 3:4], rts[:, s, 1:2], rts[:, s, 2:3], ALU.mult))
                link(nc.vector.tensor_scalar(logits, iota8[:], rts[:, s, 4:5], rts[:, s, 2:3], ALU.is_equal, ALU.mult))
                link(nc.vector.tensor_scalar(top8, iota8[:], rts[:, s, 5:6], rts[:, s, 3:4], ALU.is_equal, ALU.mult))
                link(nc.vector.tensor_tensor(logits, logits, top8, ALU.add))
                if i >= 2:
                    dve.wait_ge(s_ft, i - 1)
                nc.vector.tensor_tensor(hid[:, s, :].rearrange("p (e r) -> p e r", e=NE),
                                        ps[:, 2 + s, NE:NE + ER].rearrange("p (e r) -> p e r", e=NE),
                                        logits.unsqueeze(2).broadcast_to([P, NE, RANK]), ALU.mult).then_inc(s_hw, 1)

            def dequantise(g, c):
                if c < KC:
                    dve.wait_ge(s_wl[c], g * 96 + 96)
                    w, sc = stq[:, c, :], scale[:, c % 2, :]
                else:
                    dve.wait_ge(s_wl[c], g * 32 + 32)
                    w, sc = sto[:, c - KC, :], scale[:, c % 2, 0:D]
                nc.vector.scalar_tensor_tensor(w, w.bitcast(I32), -ZERO, sc, ALU.add, ALU.mult).then_inc(s_dq, 1)

            def mixture(q, buf):
                def add(t):
                    i = T * q + t
                    dve.wait_ge(s_fy, i + 1)
                    dve.wait_ge(s_xb, T * (q + 1) + t + 1)
                    nc.vector.tensor_tensor(buf[:, t, :], buf[:, t, :], ps[:, 4 + t % 2, :], ALU.add).then_inc(s_fx, 1)

                for t in range(T):
                    route(q, t)
                    if t >= 1:
                        add(t - 1)
                    if q == 0:
                        dequantise(0, t)
                add(T - 1)

            mixture(0, x)
            def low_tokens(t):
                dve.wait_ge(s_xt, 2 * T + t + 1)
                c = slice(t * P, (t + 1) * P)
                nc.vector.tensor_tensor(xTl[:, :, c], ps[:, t % 2, :].rearrange("p (k n) -> p k n", k=KC),
                                        xTh[:, :, c].bitcast(F32), ALU.subtract).then_inc(s_xl, 1)

            norm(2, xnat, lambda t: dve.wait_ge(s_nat[t // 2], 64), low_tokens)

            def rope_cos(v, par, t, first=False):
                dve.wait_ge(s_vb, v + 1)
                slot = v_slot(t, par)
                nc.vector.tensor_tensor(vl[:, slot, :], ps[:, 7, P:2 * P], vh[:, slot, :].bitcast(F32),
                                        ALU.subtract).then_inc(s_rope, 1)
                if not first:
                    dve.wait_ge(s_qkT, v)
                nc.vector.tensor_tensor(rc1[:].rearrange("p (h d) -> p h d", h=BH), rotary_in(),
                                        cos[:, t:t + 1, :].broadcast_to([P, BH, P]), ALU.mult).then_inc(s_rope, 1)

            def rotary_in():
                return ps[:, 6:8, :].rearrange("p b n -> p (b n)")[:, 0:BH * P].rearrange("p (h d) -> p h d", h=BH)

            def rope_sin(t):
                s = sin[:, t:t + 1, :].broadcast_to([P, BH, P])
                o = rc2[:].rearrange("p (h d) -> p h d", h=BH)
                for a, b in ((0, P // 2), (P // 2, 0)):
                    nc.vector.tensor_tensor(o[:, :, a:a + P // 2], rotary_in()[:, :, b:b + P // 2], s[:, :, a:a + P // 2],
                                            ALU.mult).then_inc(s_rope, 1)

            def maximum(u, h, n):
                dve.wait_ge(s_sc, u * R + h + 1)
                nc.vector.tensor_reduce(nmb[:, h:h + 1], flat(2 * (h % 2), n), AX.X, ALU.max, negate=True).then_inc(s_nb, 1)

            def invert(u, h):
                dve.wait_ge(s_eb, u * R + h + 1)
                nc.vector.reciprocal(rden[:, h:h + 1], den[:, h:h + 1]).then_inc(s_rd, 1)

            def weigh(u, h, n):
                dve.wait_ge(s_rd, u * R + h + 1)
                nc.vector.tensor_scalar(pr[:, h, 0:n], pr[:, h, 0:n], rden[:, h:h + 1], None, ALU.mult).then_inc(s_pd, 1)

            def turned(v, t):
                dve.wait_ge(s_qke, v * 2 + 2)
                nc.vector.scalar_tensor_tensor(qTl[:].rearrange("p h n -> p (h n)"), ps[:, 6, :], SC_B,
                                               qTh[:].rearrange("p h n -> p (h n)").bitcast(F32), ALU.mult,
                                               ALU.subtract).then_inc(s_ql, 1)
                c = slice(t * P, (t + 1) * P)
                nc.vector.tensor_tensor(kTl[:, c], ps[:, 7, 0:P], kTh[:, c].bitcast(F32), ALU.subtract).then_inc(s_ql, 1)

            def output_low(g, c):
                dve.wait_ge(s_wh, g * 8 + KC + c + 1)
                nc.vector.tensor_tensor(wol[:, c, :], sto[:, c, :], woh[:, c, :].bitcast(F32),
                                        ALU.subtract).then_inc(s_wld, 1)

            def add(v, t):
                dve.wait_ge(s_op, v + 1)
                nc.vector.tensor_tensor(xnat[:, t, :], xnat[:, t, :], ps[:, 4, :], ALU.add).then_inc(s_xo, 1)

            def front(g, par, t, last, first=False):
                u = g * T + t
                n = (t + 1) * P
                end = last and t == T - 1
                maximum(u, 0, n)
                maximum(u, 1, n)
                invert(u, 0)
                if not last:
                    for c in CHUNKS[t]:
                        dequantise(g + 1, c)
                if t == 1:
                    output_low(g, 2)
                    output_low(g, 3)
                _, p2, t2 = after(g, par, t)
                maximum(u, 2, n)
                invert(u, 1)
                maximum(u, 3, n)
                if t < LATE_VALUES and not end:
                    rope_cos(u + 1, p2, t2)
                weigh(u, 1, n)
                if t < LATE_VALUES and not end:
                    rope_sin(t2)
                invert(u, 2)
                invert(u, 3)
                weigh(u, 3, n)
                if t >= LATE_VALUES and not end:
                    rope_cos(u + 1, p2, t2)
                    rope_sin(t2)
                if t not in HALVED and not first:
                    add(u - 1, (t - 1) % T)

            def back(g, par, t, last):
                u = g * T + t
                for kt in range(t + 1):
                    dve.wait_ge(s_ph, key_tile(g, t, kt) + 1)
                    nc.vector.tensor_tensor(pTl[:, kt % PTS, :], ps[:, PT_BANK[kt % PTS], :],
                                            pTh[:, kt % PTS, :].bitcast(F32), ALU.subtract).then_inc(s_pl, 1)
                    if kt == min(t, TURN) and not (last and t == T - 1):
                        turned(u + 1, (t + 1) % T)
                if t in HALVED:
                    add(u - 1, t - 1)
                dve.wait_ge(s_ch_b, u + 1)
                nc.vector.tensor_tensor(cTl[:].rearrange("p h n -> p (h n)"), ps[:, 2, :],
                                        cTh[:].rearrange("p h n -> p (h n)").bitcast(F32), ALU.subtract).then_inc(s_cx, 1)
                if t == 0:
                    output_low(g, 0)
                    output_low(g, 1)

            dve.wait_ge(s_tab, 48)
            link(nc.vector.tensor_copy(mask[:], rc2[:, 0:P]))
            rope_cos(0, 0, 0, True)
            rope_sin(0)
            turned(0, 0)
            front(0, 0, 0, False, True)
            with dve.Fori(0, G // 2 - 1) as gg:
                for par in range(2):
                    for t in range(T):
                        back(gg * 2 + par, par, t, False)
                        front(*after(gg * 2 + par, par, t), False)
            for n in range(2 * T):
                g, par, t = G - 2 + n // T, n // T, n % T
                back(g, par, t, g == G - 1)
                if n < 2 * T - 1:
                    front(*after(g, par, t), g == G - 1 or t == T - 1)
            add(G * T - 1, T - 1)
            norm(3, xnat, lambda t: dve.wait_ge(s_xo, (G - 1) * T + t + 1))
            mixture(1, xnat)

        @block.tensor
        def _(pe):
            mm = nc.tensor.matmul

            def norm(phase):
                for t in range(T):
                    i = T * phase + t
                    pe.wait_ge(s_xh, i + 1)
                    if i >= 2:
                        pe.wait_ge(s_xt, i - 1)
                    for k in range(KC):
                        ins = nc.tensor.transpose(ps[:, i % 2, k * P:(k + 1) * P], xh[:, t % 2, k * P:(k + 1) * P], ident[:])
                    ins.then_inc(s_lntr, 1)

            pe.wait_ge(s_cst, 16)
            norm(0)
            pe.wait_ge(s_wqkv, 16 * 6)
            pe.wait_ge(s_xt, T)
            for n, j in enumerate((4, 0, 1, 2, 3)):
                if n >= 2:
                    pe.wait_ge(s_q32, 2 * n - 2)
                for c in range(2):
                    for k in range(KC):
                        lhs = wkv[:, k, 0:P] if j == 4 else wq[:, k, j * P:(j + 1) * P]
                        ins = mm(ps[:, 2 + 2 * (n % 2) + c, :], lhs, xT[:, k, c * HALF:(c + 1) * HALF],
                                 start=(k == 0), stop=(k == KC - 1))
                ins.then_inc(s_qk, 1)
                if n == 1:
                    for t in range(T):
                        for k in range(KC):
                            ins = mm(ps[:, 6 + t // 4, (t % 4) * P:(t % 4 + 1) * P], xT[:, k, t * P:(t + 1) * P],
                                     wkv[:, k, P:2 * P], start=(k == 0), stop=(k == KC - 1))
                        if t % 4 == 3:
                            ins.then_inc(s_v, 1)
            pe.wait_ge(s_raw, 16)
            for n in range(KC + 3):
                if n >= 2:
                    pe.wait_ge(s_we, n - 1)
                if n == KC:
                    pe.wait_ge(s_rawa, 16 * (2 + KC))
                for k in range(KC):
                    if n < KC:
                        src, dst = raw[:, k, n * P:(n + 1) * P], ps[:, n % 2, k * P:(k + 1) * P]
                    elif n == KC:
                        src, dst = raw[:, 0, k * P:(k + 1) * P], ps[:, n % 2, k * P:(k + 1) * P]
                    elif n == KC + 1:
                        src, dst = raw[:, 2, k * P:(k + 1) * P], ps[:, n % 2, k * P:(k + 1) * P]
                    else:
                        src, dst = raw[0:NE, 1, k * P:(k + 1) * P], ps[:, n % 2, k * NE:(k + 1) * NE]
                    ins = nc.tensor.transpose(dst, src, ident[0:src.shape[0], 0:src.shape[0]])
                ins.then_inc(s_wt, 1)

            def maxima(g, f, k0, k1, first=False):
                for k in range(k0, k1):
                    h, qt, kh = k // 8, k // 2 % 4, k % 2
                    if not (first and k < 2):
                        pe.wait_ge(s_mx, (g * 2 + f) * MM + k - 1)
                    mm(ps[:, k % 2, :], qs[0:STACK, ds(g * R + h, 1), f * HALF + qt * P:f * HALF + (qt + 1) * P],
                       ks[0:STACK, ds(g, 1), kh * HALF:(kh + 1) * HALF], start=True, stop=True).then_inc(s_mm, 1)

            def rows(g, f, r, first=False):
                u = g * 2 + f
                if r == 0:
                    pe.wait_ge(s_ch, u * 5 + 5)
                    if f == 0 and not first:
                        pe.wait_ge(s_on, u - 1)
                else:
                    pe.wait_ge(s_rw, u * 2 + 1)
                for i in range(8):
                    ins = nc.tensor.transpose(ps[STACK:STACK + NEG, 2, :].bitcast(BF16)[:, i * P:(i + 1) * P],
                                              mparts[:, 8 * r + i, 0:NEG], identb[:])
                ins.then_inc(s_rt, 1)

            def scores(g, f, kt, r, first=False):
                u = g * 2 + f
                if kt == 0 and r == 0:
                    pe.wait_ge(s_rw, u * 2 + 2)
                if not (first and kt == 0):
                    pe.wait_ge(s_ex, u * (2 * KT) + 2 * kt + r - 1)
                for j in range(2):
                    ins = mm(ps[:, 4 + 2 * r + j, :], ks[0:STACK + NEG, ds(g, 1), kt * P:(kt + 1) * P],
                             qs[0:STACK + NEG, ds(g * R + 2 * r + j, 1), f * HALF:(f + 1) * HALF],
                             start=True, stop=True)
                ins.then_inc(s_sT, 1)

            def context(g, f, kt):
                u = g * 2 + f
                pe.wait_ge(s_ex, u * (2 * KT) + 2 * kt + 2)
                if kt == 0:
                    if f == 1:
                        pe.wait_ge(s_ob, u)
                    else:
                        pe.wait_ge(s_vc, g + 1)
                for j in range(R):
                    ins = mm(ps[VW * j:VW * j + VW, 3, :], vcur[:, kt, :],
                             pbuf[:, 2 * (kt % 2) + j // 2, (j % 2) * HALF:(j % 2 + 1) * HALF],
                             start=(kt == 0), stop=(kt == KT - 1))
                ins.then_inc(s_pv, 1)

            def turn(g, f):
                pe.wait_ge(s_ob, g * 2 + f + 1)
                if f == 1:
                    pe.wait_ge(s_on, g * 2 + 1)
                for i in range(4):
                    ins = nc.tensor.transpose(ps[:, 2, i * P:(i + 1) * P], osb[:, i * P:(i + 1) * P], ident[:])
                ins.then_inc(s_ot, 1)

            def group_a(g, last):
                for f in range(2):
                    end = last and f == 1
                    for kt in range(KT):
                        if f == 1 and kt == 1:
                            turn(g, 0)
                        if kt in (3, 4) and not end:
                            rows(g + f, 1 - f, kt - 3)
                        for r in range(2):
                            if not last:
                                maxima(g + 1, f, 4 * kt + r, 4 * kt + r + 1)
                            if kt < KT - 1:
                                scores(g, f, kt + 1, r)
                            elif not end:
                                scores(g + f, 1 - f, 0, r)
                        if not last:
                            maxima(g + 1, f, 4 * kt + 2, 4 * kt + 3)
                        context(g, f, kt)
                        if not last:
                            maxima(g + 1, f, 4 * kt + 3, 4 * kt + 4)
                turn(g, 1)

            pe.wait_ge(s_we, KC + 3)
            pe.wait_ge(s_idb, 1)
            pe.wait_ge(s_stk[4], 16 * len(K_PART))
            pe.wait_ge(s_stk[0], 16 * len(K_PART))
            maxima(0, 0, 0, MM, True)
            pe.wait_ge(s_q32, 10)
            for r in range(2):
                rows(0, 0, r, True)
            maxima(0, 1, 0, MM)
            for j in range(1, 4):
                pe.wait_ge(s_stk[j], 16 * len(K_PART))
            pe.wait_ge(s_set, 5)
            pe.wait_ge(s_vx, 2)
            for r in range(2):
                scores(0, 0, 0, r, True)
            with pe.Fori(0, G - 1) as g:
                group_a(g, False)
            group_a(G - 1, True)

            pe.wait_ge(s_on, 2 * G)
            pe.wait_ge(s_wo, 16)
            for i in range(T):
                b, f = i // 2, i % 2
                if i >= 2:
                    pe.wait_ge(s_xa, i - 1)
                for c in range(4):
                    ins = mm(ps[:, i % 2, :], oall[:, 4 * f + c, b * P:(b + 1) * P], wo[:, c, :],
                             start=(c == 0), stop=(c == 3))
                ins.then_inc(s_wom, 1)
            norm(1)

            def mixture(q):
                def low_rank(t):
                    i = T * q + t
                    pe.wait_ge(s_hw, i + 1)
                    nc.tensor.transpose(ps[:, 6, 0:P], hid[:, t % 2, :], ident[:]).then_inc(s_ft, 1)
                    pe.wait_ge(s_fc, i + 1)
                    mm(ps[:, 4 + t % 2, :], hidT[:, t % 2, :], bT[:], start=False, stop=True).then_inc(s_fy, 1)

                for t in range(T):
                    i = T * q + t
                    pe.wait_ge(s_xt, T * (2 * q + 1) + t + 1)
                    if i >= 2:
                        pe.wait_ge(s_hw, i - 1)
                    for w, c0, c1 in ((wrT, 0, NE), (aT, NE, NE + ER)):
                        for k in range(KC):
                            ins = mm(ps[:, 2 + t % 2, c0:c1], xT[:, k, t * P:(t + 1) * P], w[:, k, :],
                                     start=(k == 0), stop=(k == KC - 1))
                    ins.then_inc(s_fh, 1)
                    if i >= 2:
                        pe.wait_ge(s_fx, i - 1)
                    for k in range(KC):
                        mm(ps[:, 4 + t % 2, :], xT[:, k, t * P:(t + 1) * P], wbT[:, k, :],
                           start=(k == 0), stop=False)
                    if t >= 1:
                        low_rank(t - 1)
                low_rank(T - 1)

            mixture(0)
            norm(2)

            def products(out, left, right, start, stop):
                for i, ((lh, ll), (rh, rl)) in enumerate(zip(left, right)):
                    mm(out, lh, rh, start=(start and i == 0), stop=False)
                    mm(out, lh, rl, start=False, stop=False)
                    ins = mm(out, ll, rh, start=False, stop=(stop and i == len(left) - 1))
                return ins

            def project(v, g, t, half):
                if half == 0 and t == 0:
                    pe.wait_ge(s_wlp, g * KC + KC)
                c = slice(t * P, (t + 1) * P)
                c0, c1 = ((0, R * P), (R * P, BW))[half]
                ins = products(ps[:, 6 + half, 0:c1 - c0], [(xTh[:, k, c], xTl[:, k, c]) for k in range(KC)],
                               [(wh[:, k, c0:c1], wl[:, k, c0:c1]) for k in range(KC)], True, True)
                if half == 1:
                    ins.then_inc(s_pj, 1)

            def turn_b(v):
                pe.wait_ge(s_rpa, v + 1)
                for h in range(BH):
                    dst = ps[:, 6, h * P:(h + 1) * P] if h < R else ps[:, 7, 0:P]
                    ins = nc.tensor.transpose(dst, rc1[:, h * P:(h + 1) * P], ident[:])
                ins.then_inc(s_qkT, 1)

            def output(v, heads):
                if 0 in heads:
                    pe.wait_ge(s_cx, v + 1)
                ins = products(ps[:, 4, :], [(cTh[:, h, :], cTl[:, h, :]) for h in heads],
                               [(woh[:, h, :], wol[:, h, :]) for h in heads], 0 in heads, R - 1 in heads)
                if R - 1 in heads:
                    ins.then_inc(s_op, 1)

            def front(g, par, t, last, first=False):
                u = g * T + t
                n = (t + 1) * P
                end = last and t == T - 1
                g2, _, t2 = after(g, par, t)
                pe.wait_ge(s_ql, u * 2 + 2)
                for h in range(R):
                    if h == (1 if t < SHORT else 2) and not end:
                        project(u + 1, g2, t2, 0)
                    if h == 1 and not first:
                        pe.wait_ge(s_cx, u)
                    if h == 2 and t < LATE_VALUES and not end:
                        project(u + 1, g2, t2, 1)
                    if h >= 2:
                        pe.wait_ge(s_eb, u * R + h - 1)
                    b = 2 * (h % 2)
                    for c in range(0, n, 512):
                        w = min(512, n - c)
                        diag = c + w == n
                        ins = products(ps[:, b + c // 512, 0:w], [(qTh[:, h, :], qTl[:, h, :])],
                                       [(kTh[:, c:c + w], kTl[:, c:c + w])], True, not diag)
                        if diag:
                            ins = mm(ps[:, b + c // 512, w - P:w], identb[:], mask[:], start=False, stop=True)
                    ins.then_inc(s_sc, 1)
                if t >= LATE_VALUES and not end:
                    project(u + 1, g2, t2, 1)
                if t == 1:
                    pe.wait_ge(s_wld, g * R + R)
                if not first:
                    output(u - 1, (0, 1) if t in HALVED else range(R))

            def back(g, par, t, last):
                u = g * T + t
                pe.wait_ge(s_pn, u * 2 + 2)
                pe.wait_ge(s_pd, u * 2 + 2)
                turn_at = t + 1 if t < TURN else TURN
                for kt in range(t + PTS):
                    if kt <= t:
                        if kt == PTS - 1:
                            pe.wait_ge(s_xo, u)
                        for h in range(R):
                            ins = nc.tensor.transpose(ps[:, PT_BANK[kt % PTS], h * P:(h + 1) * P],
                                                      pr[:, h, kt * P:(kt + 1) * P], ident[:])
                        ins.then_inc(s_pt, 1)
                    if kt == turn_at and not (last and t == T - 1):
                        turn_b(u + 1)
                    if kt == t + 1 and t in HALVED:
                        output(u - 1, (2, 3))
                    if kt >= PTS - 1:
                        k = kt - PTS + 1
                        slot = v_slot(k, par)
                        pe.wait_ge(s_pl, key_tile(g, t, k) + 1)
                        products(ps[:, 2, :], [(vh[:, slot, :], vl[:, slot, :])],
                                 [(pTh[:, k % PTS, :], pTl[:, k % PTS, :])], k == 0, k == t).then_inc(s_pvb, 1)

            pe.wait_ge(s_xl, T)
            project(0, 0, 0, 0)
            project(0, 0, 0, 1)
            turn_b(0)
            front(0, 0, 0, False, True)
            with pe.Fori(0, G // 2 - 1) as gg:
                for par in range(2):
                    for t in range(T):
                        back(gg * 2 + par, par, t, False)
                        front(*after(gg * 2 + par, par, t), False)
            for n in range(2 * T):
                g, par, t = G - 2 + n // T, n // T, n % T
                back(g, par, t, g == G - 1)
                if n < 2 * T - 1:
                    front(*after(g, par, t), g == G - 1 or t == T - 1)
            output(G * T - 1, range(R))
            norm(3)
            mixture(1)


_INS = ['L0_attn_a_hidden_state', 'L0_attn_a_wq', 'L0_attn_a_bq', 'L0_attn_a_wk', 'L0_attn_a_bk', 'L0_attn_a_wv',
        'L0_attn_a_bv', 'L0_attn_a_wo', 'L0_attn_a_bo', 'L0_attn_b_scales_q', 'L0_attn_b_scales_k',
        'L0_attn_b_scales_v', 'L0_attn_b_scales_o', 'L0_attn_b_qw_q', 'L0_attn_b_qw_k', 'L0_attn_b_qw_v',
        'L0_attn_b_qw_o', 'L0_ffn_W_base', 'L0_ffn_b_base', 'L0_ffn_W_router', 'L0_ffn_A', 'L0_ffn_B']


def constants():
    f = np.float32
    inv = f(1.0) / np.power(f(10000.0), np.arange(0, P, 2, dtype=f) / f(P))
    ang = np.arange(S, dtype=f)[:, None] * inv
    cos = np.concatenate([np.cos(ang), np.cos(ang)], axis=1).astype(f)
    sin = np.concatenate([-np.sin(ang), np.sin(ang)], axis=1).astype(f)
    mask = np.where(np.tril(np.ones((P, P), bool)), 0.0, -3e38).astype(f)
    return {"ident": np.eye(P, dtype=f), "cos": cos, "sin": sin, "mask": mask}


def kernel(**inputs):
    import concourse.bacc as _bacc
    from concourse.bass_utils import run_bass_kernel_spmd as _run

    nc = _bacc.Bacc("TRN2", target_bir_lowering=False, num_devices=1)
    arrays, args = {}, []
    for name, a in [(n, inputs[n]) for n in _INS] + list(constants().items()):
        a = np.ascontiguousarray(a)
        arrays[f"in_{name}_dram"] = a
        args.append(nc.dram_tensor(f"in_{name}_dram", a.shape, mybir.dt.from_np(a.dtype), kind="ExternalInput").ap())
    args.append(nc.dram_tensor("out_0_dram", (1, S, D), F32, kind="ExternalOutput").ap())
    build(nc, *args)
    r = _run(nc, [arrays], core_ids=[0])
    return r.results[0]["out_0_dram"]
```
